# Optimizing a Trainium2 kernel written in Bass

```python
import numpy as np
import jax
import jax.numpy as jnp

def _softmax(x, axis=-1):
    return jax.nn.softmax(x, axis=axis)

def _gelu(x):
    return jax.nn.gelu(x, approximate=True)

def _silu(x):
    return jax.nn.silu(x)

def _sigmoid(x):
    return jax.nn.sigmoid(x)

def _layernorm(x, axis=-1, eps=1e-05):
    m = jnp.mean(x, axis=axis, keepdims=True)
    v = jnp.var(x, axis=axis, keepdims=True)
    return (x - m) / jnp.sqrt(v + eps)

def _scatter_add(tgt, idx, src, axis=0):
    return tgt.at[idx].add(src)

def _segment_sum(src, seg, n):
    return jax.ops.segment_sum(src, seg, n)
kernel_name = 'mk_audio_tower_d1_tok_audfeat2048_r4_5bfe39'

def setup_inputs(seed: int=0):
    np.random.seed(seed)
    _w = jnp.asarray

    def _rec_inputs():
        import jax
        import jax.numpy as jnp
        _rk = jax.random.key(seed)
        x = -0.000520686 + 1.00062 * jax.random.normal(jax.random.fold_in(_rk, 1), (64, 750, 1), jnp.float32)
        return x
    x = _rec_inputs()

    def _L0_tok_setup():
        import jax, jax.numpy as jnp
        import numpy as np
        PATCH_LEN = 128
        D_MODEL = 512
        BATCH = 128
        SEQ_LEN = 4096
        FEATURES = 1
        key = jax.random.key(seed)
        k1, k2, k3 = jax.random.split(key, 3)
        x = jax.random.normal(k1, (BATCH, SEQ_LEN, FEATURES), dtype=jnp.float32)
        W = jax.random.normal(k2, (D_MODEL, PATCH_LEN), dtype=jnp.float32) * (1.0 / np.sqrt(PATCH_LEN))
        b = jax.random.normal(k3, (D_MODEL,), dtype=jnp.float32) * 0.01
        return {'x': x, 'W': W, 'b': b}
    _L0_tok_all = _L0_tok_setup()
    _L0_tok_in = {k: v for k, v in _L0_tok_all.items() if k in ('W', 'b')}
    del _L0_tok_all

    def _L0_attn_setup():
        import jax, jax.numpy as jnp
        import numpy as np
        D_MODEL = 512
        N_HEADS = 16
        N_KV = 4
        HEAD_DIM = D_MODEL // N_HEADS
        N_GROUPS = N_HEADS // N_KV
        BLOCK_SIZE = 128
        THETA = 10000.0

        def _rope_tables(T):
            freqs = 1.0 / THETA ** (jnp.arange(0, HEAD_DIM, 2, dtype=jnp.float32) / HEAD_DIM)
            t = jnp.arange(T, dtype=jnp.float32)
            emb = jnp.outer(t, freqs)
            cos = jnp.cos(emb)
            sin = jnp.sin(emb)
            return (jnp.concatenate([cos, cos], -1), jnp.concatenate([sin, sin], -1))

        def _apply_rope(x, cos, sin):
            half = HEAD_DIM // 2
            x1, x2 = (x[..., :half], x[..., half:])
            rot = jnp.concatenate([-x2, x1], -1)
            return x * cos + rot * sin
        key = jax.random.key(seed)
        ks = jax.random.split(key, 5)
        B, T = (2, 512)
        x = jax.random.normal(ks[0], (B, T, D_MODEL), dtype=jnp.float32)
        s = 0.02
        Wq = jax.random.normal(ks[1], (D_MODEL, N_HEADS * HEAD_DIM), dtype=jnp.float32) * s
        Wk = jax.random.normal(ks[2], (D_MODEL, N_KV * HEAD_DIM), dtype=jnp.float32) * s
        Wv = jax.random.normal(ks[3], (D_MODEL, N_KV * HEAD_DIM), dtype=jnp.float32) * s
        Wo = jax.random.normal(ks[4], (N_HEADS * HEAD_DIM, D_MODEL), dtype=jnp.float32) * s
        return {'x': x, 'Wq': Wq, 'Wk': Wk, 'Wv': Wv, 'Wo': Wo}
    _L0_attn_all = _L0_attn_setup()
    _L0_attn_in = {k: v for k, v in _L0_attn_all.items() if k in ('Wq', 'Wk', 'Wv', 'Wo')}
    del _L0_attn_all

    def _L0_ffn_setup():
        import jax, jax.numpy as jnp
        import numpy as np
        TOPK = 2
        N_EXPERTS = 8
        ROUTE_SCALE = 1.0
        key = jax.random.key(seed)
        ks = jax.random.split(key, 7)
        B, T, C = (4, 512, 512)
        H = 352
        HS = 704
        E = N_EXPERTS
        s = 0.02
        return {'x': jax.random.normal(ks[0], (B, T, C), jnp.float32), 'gate_w': jax.random.normal(ks[1], (E, C), jnp.float32) * s, 'gate_bias': jnp.zeros((E,), jnp.float32), 'shared_gw': jax.random.normal(ks[2], (2 * HS, C), jnp.float32) * s, 'shared_dw': jax.random.normal(ks[3], (C, HS), jnp.float32) * s, 'up_w': jax.random.normal(ks[4], (E, 2 * H, C), jnp.float32) * s, 'down_w': jax.random.normal(ks[5], (E, C, H), jnp.float32) * s}
    _L0_ffn_all = _L0_ffn_setup()
    _L0_ffn_in = {k: v for k, v in _L0_ffn_all.items() if k in ('gate_w', 'gate_bias', 'shared_gw', 'shared_dw', 'up_w', 'down_w')}
    del _L0_ffn_all
    return {'x': x, 'L0_tok_W': _L0_tok_in['W'], 'L0_tok_b': _L0_tok_in['b'], 'L0_attn_Wq': _L0_attn_in['Wq'], 'L0_attn_Wk': _L0_attn_in['Wk'], 'L0_attn_Wv': _L0_attn_in['Wv'], 'L0_attn_Wo': _L0_attn_in['Wo'], 'L0_ffn_gate_w': _L0_ffn_in['gate_w'], 'L0_ffn_gate_bias': _L0_ffn_in['gate_bias'], 'L0_ffn_shared_gw': _L0_ffn_in['shared_gw'], 'L0_ffn_shared_dw': _L0_ffn_in['shared_dw'], 'L0_ffn_up_w': _L0_ffn_in['up_w'], 'L0_ffn_down_w': _L0_ffn_in['down_w']}

def reference(x, L0_tok_W, L0_tok_b, L0_attn_Wq, L0_attn_Wk, L0_attn_Wv, L0_attn_Wo, L0_ffn_gate_w, L0_ffn_gate_bias, L0_ffn_shared_gw, L0_ffn_shared_dw, L0_ffn_up_w, L0_ffn_down_w):
    import jax
    import jax.numpy as jnp

    def _L0_tok_ref(x, W, b):
        import jax, jax.numpy as jnp
        import numpy as np
        PATCH_LEN = 128
        D_MODEL = 512
        BATCH = 128
        SEQ_LEN = 4096
        FEATURES = 1
        B, S, F = x.shape
        P = PATCH_LEN
        stride = P // 2
        starts = jnp.arange(0, S - P + 1, stride)
        idx = starts[:, None] + jnp.arange(P)
        patches = x[:, idx, :].reshape(B, starts.shape[0], P * F)
        patches = patches[:, :, :P]
        return jnp.einsum('bnp,dp->bnd', patches, W) + b

    def _L0_attn_ref(x, Wq, Wk, Wv, Wo):
        import jax, jax.numpy as jnp
        import numpy as np
        D_MODEL = 512
        N_HEADS = 16
        N_KV = 4
        HEAD_DIM = D_MODEL // N_HEADS
        N_GROUPS = N_HEADS // N_KV
        BLOCK_SIZE = 128
        THETA = 10000.0

        def _rope_tables(T):
            freqs = 1.0 / THETA ** (jnp.arange(0, HEAD_DIM, 2, dtype=jnp.float32) / HEAD_DIM)
            t = jnp.arange(T, dtype=jnp.float32)
            emb = jnp.outer(t, freqs)
            cos = jnp.cos(emb)
            sin = jnp.sin(emb)
            return (jnp.concatenate([cos, cos], -1), jnp.concatenate([sin, sin], -1))

        def _apply_rope(x, cos, sin):
            half = HEAD_DIM // 2
            x1, x2 = (x[..., :half], x[..., half:])
            rot = jnp.concatenate([-x2, x1], -1)
            return x * cos + rot * sin
        B, T, C = x.shape
        q = (x @ Wq).reshape(B, T, N_HEADS, HEAD_DIM).transpose(0, 2, 1, 3)
        k = (x @ Wk).reshape(B, T, N_KV, HEAD_DIM).transpose(0, 2, 1, 3)
        v = (x @ Wv).reshape(B, T, N_KV, HEAD_DIM).transpose(0, 2, 1, 3)
        cos, sin = _rope_tables(T)
        q = _apply_rope(q, cos, sin)
        k = _apply_rope(k, cos, sin)
        qg = q.reshape(B, N_KV, N_GROUPS, T, HEAD_DIM)
        scale = 1.0 / jnp.sqrt(jnp.float32(HEAD_DIM))
        scores = jnp.einsum('bngtd,bnsd->bngts', qg, k) * scale
        blk = jnp.arange(T) // BLOCK_SIZE
        masked = blk[None, :] > blk[:, None]
        scores = jnp.where(masked, -jnp.inf, scores)
        attn = jax.nn.softmax(scores, axis=-1)
        y = jnp.einsum('bngts,bnsd->bngtd', attn, v)
        y = y.reshape(B, N_HEADS, T, HEAD_DIM).transpose(0, 2, 1, 3).reshape(B, T, C)
        return y @ Wo

    def _L0_ffn_ref(x, gate_w, gate_bias, shared_gw, shared_dw, up_w, down_w):
        import jax, jax.numpy as jnp
        import numpy as np
        TOPK = 2
        N_EXPERTS = 8
        ROUTE_SCALE = 1.0
        B, T, C = x.shape
        xf = x.reshape(-1, C)
        yg = xf @ shared_gw.T
        y, g = jnp.split(yg, 2, axis=-1)
        shared = jax.nn.silu(g) * y @ shared_dw.T
        scores = jax.nn.sigmoid(xf @ gate_w.T)
        _, topk_idx = jax.lax.top_k(scores + gate_bias, TOPK)
        w = jnp.take_along_axis(scores, topk_idx, axis=-1)
        w = w / jnp.sum(w, axis=-1, keepdims=True) * ROUTE_SCALE
        out = jnp.zeros_like(xf)
        for e in range(N_EXPERTS):
            we = jnp.sum(jnp.where(topk_idx == e, w, 0.0), axis=-1)
            gu = xf @ up_w[e].T
            g_e, u_e = jnp.split(gu, 2, axis=-1)
            h = jax.nn.silu(g_e) * u_e
            out = out + h @ down_w[e].T * we[:, None]
        return (shared + out).reshape(B, T, C)
    h = _L0_tok_ref(x, L0_tok_W, L0_tok_b)
    h = h + _L0_attn_ref(_layernorm(h, axis=-1), L0_attn_Wq, L0_attn_Wk, L0_attn_Wv, L0_attn_Wo)
    h = h + _L0_ffn_ref(_layernorm(h, axis=-1), L0_ffn_gate_w, L0_ffn_gate_bias, L0_ffn_shared_gw, L0_ffn_shared_dw, L0_ffn_up_w, L0_ffn_down_w)
    return h

_drawn_inputs = setup_inputs


def setup_inputs(seed=0):
    import zlib

    import numpy as np

    out = dict(_drawn_inputs(seed))
    spreads = {'L0_ffn_gate_bias': (0.0, 0.301)}
    factors = {'L0_tok_b': 5.427, 'L0_attn_Wq': 4.295, 'L0_attn_Wk': 4.24}
    for name, (base, spread) in spreads.items():
        noise = np.random.default_rng([zlib.crc32(name.encode()), seed]).standard_normal(out[name].shape)
        drawn = base * np.exp(spread * noise) if base else spread * noise
        out[name] = jnp.asarray(drawn.astype(out[name].dtype))
    for name, factor in factors.items():
        out[name] = (out[name] * factor).astype(out[name].dtype)
    return out
```

```python
from contextlib import ExitStack

import numpy as np

import concourse.bass as bass
from concourse import mybir
from concourse.alu_op_type import AluOpType as ALU

F32 = mybir.dt.float32
BF16 = mybir.dt.bfloat16
I32 = mybir.dt.int32
U32 = mybir.dt.uint32
ACT = mybir.ActivationFunctionType
AX = mybir.AxisListType

P = 128
BATCH, SEQ = 64, 750
PATCH, STRIDE = 128, 64
NPOS = (SEQ - PATCH) // STRIDE + 1
TOK = BATCH * NPOS
D = 512
KC = D // P
TT = TOK // P
NKV, NGRP, HD = 4, 4, 32
THETA = 10000.0
EPS = 1e-5

AB = [11, 11, 11, 11, 10, 10]
AT = len(AB)
AW = [n * NPOS for n in AB]
A0 = [sum(AW[:a]) for a in range(AT)]
WMAX = max(AW)
NEG = -1e30

E = 8
H = 352
SH = 2
HC = [P, P, H - 2 * P]
UPW = KC * 2 * H
WA = UPW + 2 * D
SLOT = UPW + 3 * D
NSLOT = SH + E
NB = (2 * TOK + E * (P - 1)) // P
EARLY = 3
J0 = SH * EARLY
J1 = J0 + NB
JN = J1 + SH * (TT - EARLY)
FIRST_FRONT = 5

C_ID, C_TRI, C_ONE, C_MASK = 0, P, 2 * P, 3 * P
C_REV = C_MASK + WMAX
C_THR = C_REV + E
C_BLK = C_THR + TT
C_ROPE = C_BLK + NB
C_END = C_ROPE + TT * 2 * HD


def build(nc, xT, tok_w, tok_b, consts, wqkv, wo, gate_w, gate_b, wa, wb, out):
    x_disp = nc.dram_tensor("x_disp", [NB * P, D], F32, kind="Internal").ap()
    y_disp = nc.dram_tensor("y_disp", [NB * P, D], F32, kind="Internal").ap()
    out_rows = out.rearrange("b n d -> (b n) d")

    ctx = ExitStack()
    with ctx:
        def sb(name, shape, dt=F32):
            return ctx.enter_context(nc.sbuf_tensor(name, shape, dt))

        def sem(name):
            return ctx.enter_context(nc.semaphore(name))

        W = sb("weights", [P, NSLOT * SLOT])
        hres = sb("hres", [P, TT, D])
        xn2T = sb("xn2T", [P, KC, TOK])
        xb = sb("xb", [P, D])
        xbT = sb("xbT", [P, 2, KC, P])
        hg = sb("hg", [P, 2, H])
        hT = sb("hT", [P, 3, P])
        yb = sb("yb", [P, D])
        cst = sb("cst", [P, C_ROPE])
        identb = sb("identb", [P, P], BF16)
        maskb = sb("maskb", [P, WMAX], BF16)
        gw = sb("gw", [P, KC, E])
        gb = sb("gb", [P, E])
        halfneg = sb("halfneg", [P, 1])
        stats = sb("stats", [P, 2, 6])
        mv = sb("mv", [P, TT, 2])
        rstd = sb("rstd", [P, TT])
        nmax = sb("nmax", [P, NKV, NGRP])
        esum = sb("esum", [P, NKV, NGRP])
        rden = sb("rden", [P, NKV, NGRP])
        slot_i = sb("slot_i", [P, 2, TT], I32)
        wtop = sb("wtop", [P, 2, TT])
        blk = sb("blk", [1, NB], I32)
        ps = ctx.enter_context(nc.psum_tensor("ps", [P, 8, 512], F32))

        ident = cst[:, C_ID:C_ID + P]
        tri = cst[:, C_TRI:C_TRI + P]
        ones = cst[:, C_ONE:C_ONE + P]
        rev = cst[:, C_REV:C_REV + E]
        thr = cst[:, C_THR:C_THR + TT]
        blki = cst[:, C_BLK:C_BLK + NB]

        at = [FIRST_FRONT * SLOT]

        def front(n):
            at[0] += n
            return W[:, at[0] - n:at[0]]

        praw = front(NPOS * BATCH)
        pT = front(TOK)
        ropeA, ropeB = praw, pT
        tokw = front(D)
        tokb = front(D)
        rope = front(TT * 2 * HD).rearrange("p (i c d) -> p i c d", i=TT, c=2)
        wqkv_sb = front(KC * 768).rearrange("p (k n) -> p k n", k=KC)
        wo_sb = front(NGRP * D).rearrange("p (g n) -> p g n", g=NGRP)
        qkr = [front(640) for _ in range(2)]
        xnT = front(KC * TOK).rearrange("p (k t) -> p k t", k=KC)
        yT = xnT
        QT = front(NGRP * TOK).rearrange("p (g t) -> p g t", g=NGRP)
        KT = front(TOK)
        V = front(AT * P).rearrange("p (a d) -> p a d", a=AT)
        PT = [front(NGRP * WMAX) for _ in range(2)]
        assert at[0] <= (NSLOT - 1) * SLOT
        at[0] = (NSLOT - 1) * SLOT
        xn = front(TT * D).rearrange("p (i d) -> p i d", i=TT)
        prob_at = at[0]
        prob = front(NKV * NGRP * WMAX).rearrange("p (n c) -> p n c", n=NKV)
        assert at[0] <= NSLOT * SLOT
        at[0] = prob_at

        def routing(n):
            return front(n)

        sc, sbias, t0, t1, sel1, sel2, msel, pos = (routing(TT * E) for _ in range(8))
        m1, m2, r1, r2, wsum = (routing(TT) for _ in range(5))
        cnt, nblk, incl, base0 = (routing(E) for _ in range(4))
        over = routing(E * TT)
        baseT = routing(TT * E)
        blkc = routing(NB * E)
        blkf = routing(NB)
        slotf = routing(2 * TT)
        assert at[0] <= NSLOT * SLOT
        yg = W[:, SH * SLOT:SH * SLOT + 2 * TT * D].rearrange("p (c i d) -> p c i d", c=2, i=TT)

        l_x, l_tokw, l_tokb, l_cst, l_rope = (sem(n) for n in ("l_x", "l_tokw", "l_tokb", "l_cst", "l_rope"))
        l_qkv, l_wo, l_gate = sem("l_qkv"), sem("l_wo"), sem("l_gate")
        l_slot = [sem(f"l_slot{s}") for s in range(NSLOT)]
        zeroed, scattered, xb_loaded = sem("zeroed"), sem("scattered"), sem("xb_loaded")
        y_stored, gathered, out_stored = sem("y_stored"), sem("gathered"), sem("out_stored")
        (tok_done, xnT_ps, qk_done, ropeT_ps, v_done, s_done, pT_ps, pv_done, wo_done, x2T_ps, logit_done,
         rank_done, g_done, u_done, hT_ps, y_done, xbT_ps) = (sem(n) for n in (
             "tok_done", "xnT_ps", "qk_done", "ropeT_ps", "v_done", "s_done", "pT_ps", "pv_done", "wo_done",
             "x2T_ps", "logit_done", "rank_done", "g_done", "u_done", "hT_ps", "y_done", "xbT_ps"))
        (bf_ready, xnT_ready, qkT_ready, v_ready, exp_done, yT_ready, x2T_ready, sig_done, silu_done,
         hT_ready, xbT_ready) = (sem(n) for n in (
             "bf_ready", "xnT_ready", "qkT_ready", "v_ready", "exp_done", "yT_ready", "x2T_ready", "sig_done",
             "silu_done", "hT_ready", "xbT_ready"))
        (patch_ready, tok_used, stats_ready, xn_ready, rope_ready, max_done, rden_ready, pT_ready, xn2_ready,
         sel_ready, slot_ready, blk_ready, h_done, y_used, out_ready, dve_step) = (sem(n) for n in (
             "patch_ready", "tok_used", "stats_ready", "xn_ready", "rope_ready", "max_done", "rden_ready",
             "pT_ready", "xn2_ready", "sel_ready", "slot_ready", "blk_ready", "h_done", "y_used", "out_ready",
             "dve_step"))
        const_ready, zero_ready, rstd_ready, qkr_ready, prob_ready, pool_step = (sem(n) for n in (
            "const_ready", "zero_ready", "rstd_ready", "qkr_ready", "prob_ready", "pool_step"))

        def up(s, k, half):
            o = s * SLOT + k * 2 * H + half * H
            return W[:, o:o + H]

        def down(s, c):
            o = s * SLOT + UPW + c * D
            return W[0:HC[c], o:o + D]

        def y_unit(j):
            return j // SH if j < J0 else EARLY + j - J0 if j < J1 else EARLY + NB + (j - J1) // SH

        block = ctx.enter_context(nc.Block())

        @block.sync
        def _(sp):
            sp.dma_start(praw.rearrange("p (n b) -> p n b", n=NPOS),
                         bass.AP(xT.tensor, 0, [[BATCH, P], [STRIDE * BATCH, NPOS], [1, BATCH]])).then_inc(l_x, 16)
            sp.dma_start(tokw, tok_w).then_inc(l_tokw, 16)
            sp.dma_start(tokb, bass.AP(tok_b.tensor, 0, [[0, P], [1, D]])).then_inc(l_tokb, 16)
            sp.dma_start(wqkv_sb, wqkv).then_inc(l_qkv, 16)
            sp.dma_start(wo_sb, wo).then_inc(l_wo, 16)
            sp.dma_start(gw[:], gate_w).then_inc(l_gate, 16)
            sp.dma_start(gb[:], bass.AP(gate_b.tensor, 0, [[0, P], [1, E]])).then_inc(l_gate, 16)

            def load_slot(s):
                sp.dma_start(W[:, s * SLOT:s * SLOT + WA], wa[s]).then_inc(l_slot[s], 16)
                sp.dma_start(W[0:HC[2], s * SLOT + WA:(s + 1) * SLOT], wb[s]).then_inc(l_slot[s], 16)

            for s in range(FIRST_FRONT):
                load_slot(s)
            sp.wait_ge(zero_ready, 1)
            sp.dma_start(x_disp.rearrange("(b p) d -> p b d", p=P),
                         bass.AP(xb, 0, [[D, P], [0, NB], [1, D]])).then_inc(zeroed, 16)
            sp.wait_ge(wo_done, TT)
            for s in range(FIRST_FRONT, NSLOT - 1):
                load_slot(s)
            sp.wait_ge(scattered, 2 * TT * 16)
            sp.wait_ge(blk_ready, 1)
            sp.dma_start(xb[:], x_disp[0:P, :]).then_inc(xb_loaded, 16)
            load_slot(NSLOT - 1)
            sp.wait_ge(xbT_ps, 1)
            sp.dma_start(xb[:], x_disp[P:2 * P, :]).then_inc(xb_loaded, 16)

            def store_y(b):
                sp.wait_ge(y_used, b + (EARLY + 1))
                sp.dma_start(y_disp[bass.ds(b * P, P), :], yb[:]).then_inc(y_stored, 16)

            with sp.Fori(2, NB) as b:
                sp.wait_ge(xbT_ps, b)
                sp.dma_start(xb[:], x_disp[bass.ds(b * P, P), :]).then_inc(xb_loaded, 16)
                store_y(b - 2)
            store_y(NB - 2)
            store_y(NB - 1)
            for i in range(TT):
                sp.wait_ge(out_ready, i + 1)
                sp.dma_start(out_rows[i * P:(i + 1) * P, :], hres[:, i, :]).then_inc(out_stored, 16)
            sp.wait_ge(out_stored, TT * 16)

        @block.tensor
        def _(pe):
            mm = nc.tensor.matmul

            def transposes(dst, srcs, ident_ap):
                for o, src in zip(dst, srcs):
                    last = nc.tensor.transpose(o, src, ident_ap)
                return last

            pe.wait_ge(patch_ready, 1)
            pe.wait_ge(l_tokw, 16)
            for i in range(TT):
                if i >= 2:
                    pe.wait_ge(tok_used, i - 1)
                mm(ps[:, i % 2, :], pT[:, i * P:(i + 1) * P], tokw, start=True, stop=True).then_inc(tok_done, 1)

            def norm_T(i):
                pe.wait_ge(xn_ready, i + 1)
                pe.wait_ge(l_cst, 16)
                if i >= 2:
                    pe.wait_ge(xnT_ready, i - 1)
                b = 2 + i % 2
                transposes([ps[:, b, k * P:(k + 1) * P] for k in range(KC)],
                           [xn[:, i, k * P:(k + 1) * P] for k in range(KC)], ident).then_inc(xnT_ps, 1)

            def project(i):
                pe.wait_ge(xnT_ready, i + 1)
                pe.wait_ge(l_qkv, 16)
                if i >= 2:
                    pe.wait_ge(qkT_ready, i - 1)
                b = 4 + 2 * (i % 2)
                for c, n0, n1 in ((0, 0, 512), (1, 512, 640)):
                    for k in range(KC):
                        last = mm(ps[:, b + c, 0:n1 - n0], xnT[:, k, i * P:(i + 1) * P], wqkv_sb[:, k, n0:n1],
                                  start=(k == 0), stop=(k == KC - 1))
                last.then_inc(qk_done, 1)

            def rope_T(i):
                pe.wait_ge(qkr_ready, i + 1)
                b = 4 + 2 * (i % 2)
                r = qkr[i % 2]
                transposes([ps[:, b + c // 4, (c % 4) * P:(c % 4 + 1) * P] for c in range(5)],
                           [r[:, c * P:(c + 1) * P] for c in range(5)], ident).then_inc(ropeT_ps, 1)

            def values(a):
                if a < 2:
                    pe.wait_ge(tok_used, TT)
                else:
                    pe.wait_ge(v_ready, a - 1)
                for k in range(KC):
                    last = mm(ps[0:AW[a], a % 2, 0:P], xnT[:, k, A0[a]:A0[a] + AW[a]], wqkv_sb[:, k, 640:768],
                              start=(k == 0), stop=(k == KC - 1))
                last.then_inc(v_done, 1)

            norm_T(0)
            project(0)
            norm_T(1)
            project(1)
            for i in range(TT):
                rope_T(i)
                if i < TT - 1:
                    values(i)
                if i + 2 < TT:
                    norm_T(i + 2)
                    project(i + 2)
            values(TT - 1)
            values(TT)

            def scores(a):
                w = AW[a]
                for n in range(NKV):
                    if a >= 1:
                        pe.wait_ge(exp_done, 4 * (a - 1) + n + 1)
                    mm(ps[0:w, n, 0:NGRP * w], identb[0:w, 0:w],
                       maskb[0:w, 0:w].unsqueeze(1).to_broadcast([w, NGRP, w]), start=True, stop=False)
                for g in range(NGRP):
                    for n in range(NKV):
                        r = slice(n * HD, (n + 1) * HD)
                        m = mm(ps[0:w, n, g * w:(g + 1) * w], QT[r, g, A0[a]:A0[a] + w], KT[r, A0[a]:A0[a] + w],
                               start=False, stop=(g == NGRP - 1))
                        if g == NGRP - 1:
                            m.then_inc(s_done, 1)

            def prob_T(a, n):
                w, u = AW[a], 4 * a + n
                pe.wait_ge(prob_ready, u + 1)
                if u >= 2:
                    pe.wait_ge(pT_ready, u - 1)
                transposes([ps[0:w, 4 + n % 2, g * w:(g + 1) * w] for g in range(NGRP)],
                           [prob[0:w, n, g * w:(g + 1) * w] for g in range(NGRP)], ident[0:w, 0:w]).then_inc(pT_ps, 1)

            def prob_v(a, n):
                w, u = AW[a], 4 * a + n
                pe.wait_ge(pT_ready, u + 1)
                if n == 0 and a >= 1:
                    pe.wait_ge(yT_ready, a)
                mm(ps[n * HD:(n + 1) * HD, 6, 0:NGRP * w], V[0:w, a, n * HD:(n + 1) * HD], PT[n % 2][0:w, 0:NGRP * w],
                   start=True, stop=True).then_inc(pv_done, 1)

            def attend(a):
                prob_T(a, 0)
                for n in range(NKV):
                    if n + 1 < NKV:
                        prob_T(a, n + 1)
                    prob_v(a, n)

            def out_proj(i):
                pe.wait_ge(yT_ready, min(i + 2, AT))
                pe.wait_ge(l_wo, 16)
                if i >= 1:
                    pe.wait_ge(x2T_ready, i)
                for g in range(NGRP):
                    last = mm(ps[:, 7, :], yT[:, g, i * P:(i + 1) * P], wo_sb[:, g, :],
                              start=(g == 0), stop=(g == NGRP - 1))
                last.then_inc(wo_done, 1)

            def norm2_T(i):
                pe.wait_ge(xn2_ready, i + 1)
                transposes([ps[:, 7, k * P:(k + 1) * P] for k in range(KC)],
                           [xn[:, i, k * P:(k + 1) * P] for k in range(KC)], ident).then_inc(x2T_ps, 1)

            pe.wait_ge(v_ready, AT)
            pe.wait_ge(xnT_ready, TT)
            pe.wait_ge(qkT_ready, TT)
            pe.wait_ge(bf_ready, 1)
            for a in range(AT):
                scores(a)
                if a >= 1:
                    attend(a - 1)
                if a >= 3:
                    if a >= 4:
                        norm2_T(a - 4)
                    out_proj(a - 3)
            attend(AT - 1)
            norm2_T(2)
            out_proj(3)
            norm2_T(3)
            out_proj(4)
            norm2_T(4)

            pe.wait_ge(l_gate, 32)
            pe.wait_ge(yT_ready, AT)
            pe.wait_ge(x2T_ready, TT)
            for i in range(TT):
                for k in range(KC):
                    last = mm(ps[:, 6, i * E:(i + 1) * E], xn2T[:, k, i * P:(i + 1) * P], gw[:, k, :],
                              start=(k == 0), stop=(k == KC - 1))
            last.then_inc(logit_done, 1)

            def gate_up(j, par, half, xk, w):
                if half == 0:
                    pe.wait_ge(h_done, j - 1) if not isinstance(j, int) or j >= 2 else pe.wait_ge(exp_done, NKV * AT)
                for k in range(KC):
                    last = mm(ps[:, 2 * par + half, 0:H], xk(k), w(k, half), start=(k == 0), stop=(k == KC - 1))
                last.then_inc(u_done if half else g_done, 1)

            def hidden_T(j, par):
                pe.wait_ge(h_done, j + 1)
                for c in range(3):
                    last = nc.tensor.transpose(ps[0:HC[c], 4, c * P:(c + 1) * P], hg[:, par, c * P:c * P + HC[c]], ident)
                last.then_inc(hT_ps, 1)

            def down_proj(j, w, first=True, final=True, y_free=None):
                pe.wait_ge(hT_ready, j + 1)
                if y_free is not None:
                    pe.wait_ge(y_used, y_free)
                for c in range(3):
                    last = mm(ps[:, 5, :], hT[0:HC[c], c, :], w(c), start=(first and c == 0), stop=(final and c == 2))
                if final:
                    last.then_inc(y_done, 1)

            def block_T(b, last_b=False):
                pe.wait_ge(xb_loaded, (b + 1) * 16)
                transposes([ps[:, 7, k * P:(k + 1) * P] for k in range(KC)],
                           [xb[:, k * P:(k + 1) * P] for k in range(KC)], ident).then_inc(xbT_ps, 1)

            def shared_tile(j):
                return j // SH if j < J0 else EARLY + (j - J1) // SH

            def shared_x(j):
                i = shared_tile(j)
                return lambda k: xn2T[:, k, i * P:(i + 1) * P]

            def shared_down(j):
                s = (j - (0 if j < J0 else J1)) % SH
                u = y_unit(j)
                down_proj(j, lambda c: down(s, c), first=(s == 0), final=(s == SH - 1),
                          y_free=u if s == 0 and u > 0 else None)

            def shared_step(j, tail):
                s = (j - (0 if j < J0 else J1)) % SH
                if j < SH:
                    pe.wait_ge(l_slot[s], 32)
                gate_up(j, j % 2, 0, shared_x(j), lambda k, half: up(s, k, half))
                if j > 0:
                    hidden_T(j - 1, (j - 1) % 2)
                gate_up(j, j % 2, 1, shared_x(j), lambda k, half: up(s, k, half))
                if j > 0:
                    tail(j - 1)

            for j in range(J0):
                shared_step(j, shared_down)
                if j == 0:
                    pe.wait_ge(sel_ready, 1)
                    mm(ps[:, 7, 0:TT * E], tri, msel, start=True, stop=True)
                    mm(ps[:, 7, TT * E:2 * TT * E], ones, msel, start=True, stop=True).then_inc(rank_done, 1)

            def expert_of(b):
                return pe.value_load(blk[0:1, bass.ds(b, 1)] if not isinstance(b, int) else blk[0:1, b:b + 1],
                                     min_val=0, max_val=E - 1)

            def expert_up(e):
                return lambda k, half: W[:, bass.ds(e * SLOT + (SH * SLOT + k * 2 * H + half * H), H)]

            def expert_down(e):
                return lambda c: W[0:HC[c], bass.ds(e * SLOT + (SH * SLOT + UPW + c * D), D)]

            def expert_step(b, par, e, e_before, more):
                j = b + J0
                xk = lambda k: xbT[:, par, k, :]
                pe.wait_ge(xbT_ready, b + 1)
                gate_up(j, par, 0, xk, expert_up(e))
                hidden_T(j - 1, 1 - par)
                if more:
                    block_T(b + 1)
                gate_up(j, par, 1, xk, expert_up(e))
                down_proj(j - 1, expert_down(e_before), y_free=EARLY + b - 1)

            pe.wait_ge(slot_ready, 1)
            block_T(0)
            pe.wait_ge(blk_ready, 1)
            for s in range(SH, NSLOT):
                pe.wait_ge(l_slot[s], 32)
            e = expert_of(0)
            pe.wait_ge(xbT_ready, 1)
            gate_up(J0, 0, 0, lambda k: xbT[:, 0, k, :], expert_up(e))
            hidden_T(J0 - 1, 1)
            block_T(1)
            gate_up(J0, 0, 1, lambda k: xbT[:, 0, k, :], expert_up(e))
            shared_down(J0 - 1)
            with pe.Fori(1, NB - 2, 2) as b:
                for u in range(2):
                    expert_step(b + u, (1 + u) % 2, expert_of(b + u), expert_of(b + u - 1), True)
            for b in (NB - 2, NB - 1):
                expert_step(b, b % 2, expert_of(b), expert_of(b - 1), b < NB - 1)
            e_last = expert_of(NB - 1)

            def last_expert_down(j):
                down_proj(j, expert_down(e_last), y_free=EARLY + NB - 1)

            for j in range(J1, JN):
                shared_step(j, last_expert_down if j == J1 else shared_down)
            hidden_T(JN - 1, (JN - 1) % 2)
            shared_down(JN - 1)

        @block.scalar
        def _(act):
            act.dma_start(cst[:], consts[:, 0:C_ROPE]).then_inc(l_cst, 16)
            act.dma_start(rope, consts[:, C_ROPE:C_END].rearrange("p (i c d) -> p i c d", i=TT, c=2)).then_inc(l_rope, 16)
            copy = nc.scalar.copy
            act.wait_ge(l_cst, 16)
            copy(identb[:], ident)
            copy(maskb[0:WMAX, :], cst[0:WMAX, C_MASK:C_MASK + WMAX]).then_inc(bf_ready, 1)

            def norm_T(i):
                act.wait_ge(xnT_ps, i + 1)
                copy(xnT[:, :, i * P:(i + 1) * P], ps[:, 2 + i % 2, :].rearrange("p (k t) -> p k t", k=KC))\
                    .then_inc(xnT_ready, 1)

            def rope_T(i):
                act.wait_ge(ropeT_ps, i + 1)
                b = 4 + 2 * (i % 2)
                copy(QT[:, :, i * P:(i + 1) * P], ps[:, b, :].rearrange("p (g t) -> p g t", g=NGRP))
                copy(KT[:, i * P:(i + 1) * P], ps[:, b + 1, 0:P]).then_inc(qkT_ready, 1)

            def values(a):
                act.wait_ge(v_done, a + 1)
                copy(V[0:AW[a], a, :], ps[0:AW[a], a % 2, 0:P]).then_inc(v_ready, 1)

            norm_T(0)
            norm_T(1)
            for i in range(TT):
                rope_T(i)
                if i < TT - 1:
                    values(i)
                if i + 2 < TT:
                    norm_T(i + 2)
            values(TT - 1)
            values(TT)

            def exps(a, n):
                w, u = AW[a], 4 * a + n
                act.wait_ge(max_done, u + 1)
                if a >= 1:
                    act.wait_ge(pT_ps, u - 3)
                for g in range(NGRP):
                    c = slice(g * w, (g + 1) * w)
                    m = nc.scalar.activation(prob[0:w, n, c], ps[0:w, n, c], ACT.Exp, bias=nmax[0:w, n, g:g + 1],
                                             scale=1.0, accum_out=esum[0:w, n, g:g + 1])
                m.then_inc(exp_done, 1)

            def values_out(a):
                w = AW[a]
                act.wait_ge(pv_done, 4 * (a + 1))
                copy(yT[:, :, A0[a]:A0[a] + w], ps[:, 6, 0:NGRP * w].rearrange("p (g t) -> p g t", g=NGRP))\
                    .then_inc(yT_ready, 1)

            def norm2_T(i):
                act.wait_ge(x2T_ps, i + 1)
                copy(xn2T[:, :, i * P:(i + 1) * P], ps[:, 7, :].rearrange("p (k t) -> p k t", k=KC))\
                    .then_inc(x2T_ready, 1)

            for a in range(AT):
                for n in range(NKV):
                    exps(a, n)
                if a >= 1:
                    values_out(a - 1)
                if a >= 4:
                    norm2_T(a - 4)
            values_out(AT - 1)
            for i in (2, 3, 4):
                norm2_T(i)

            act.wait_ge(logit_done, 1)
            nc.scalar.activation(sc, ps[:, 6, 0:TT * E], ACT.Sigmoid).then_inc(sig_done, 1)

            def silu(j, par):
                act.wait_ge(g_done, j + 1)
                nc.scalar.activation(hg[:, par, :], ps[:, 2 * par, 0:H], ACT.Silu).then_inc(silu_done, 1)

            def hidden_T(j):
                act.wait_ge(hT_ps, j + 1)
                copy(hT[:, 0:2, :], ps[:, 4, 0:2 * P].rearrange("p (c t) -> p c t", c=2))
                copy(hT[0:HC[2], 2, :], ps[0:HC[2], 4, 2 * P:3 * P]).then_inc(hT_ready, 1)

            def block_T(b, par):
                act.wait_ge(xbT_ps, b + 1)
                copy(xbT[:, par, :, :], ps[:, 7, :].rearrange("p (k t) -> p k t", k=KC)).then_inc(xbT_ready, 1)

            for j in range(J0):
                if j > 0:
                    hidden_T(j - 1)
                silu(j, j % 2)
            block_T(0, 0)
            hidden_T(J0 - 1)
            block_T(1, 1)
            silu(J0, 0)
            with act.Fori(1, NB - 2, 2) as b:
                for u in range(2):
                    hidden_T(b + (u + J0 - 1))
                    block_T(b + (u + 1), u % 2)
                    silu(b + (u + J0), (1 + u) % 2)
            for b in (NB - 2, NB - 1):
                hidden_T(b + J0 - 1)
                if b < NB - 1:
                    block_T(b + 1, (b + 1) % 2)
                silu(b + J0, b % 2)
            for j in range(J1, JN):
                hidden_T(j - 1)
                silu(j, j % 2)
            hidden_T(JN - 1)

        @block.vector
        def _(dve):
            v = nc.vector
            steps = [0]

            def link(ins):
                steps[0] += 1
                ins.then_inc(dve_step, 1)
                dve.wait_ge(dve_step, steps[0])

            dve.wait_ge(l_x, 16)
            v.tensor_copy(pT.rearrange("p (b n) -> p b n", n=NPOS), praw.rearrange("p (n b) -> p b n", n=NPOS))\
                .then_inc(patch_ready, 1)

            def mean_var(i):
                link(v.bn_stats(stats[:, i % 2, :], hres[:, i, :]))
                v.bn_aggr(mv[:, i, :], stats[:, i % 2, :]).then_inc(stats_ready, 1)

            def embed(i):
                dve.wait_ge(tok_done, i + 1)
                if i == 0:
                    dve.wait_ge(l_tokb, 16)
                v.tensor_tensor(hres[:, i, :], ps[:, i % 2, :], tokb, ALU.add).then_inc(tok_used, 1)
                dve.wait_ge(tok_used, i + 1)
                mean_var(i)

            def normed(i, nth, done):
                dve.wait_ge(rstd_ready, nth + 1)
                v.tensor_scalar(xn[:, i, :], hres[:, i, :], mv[:, i, 0:1], rstd[:, i:i + 1],
                                ALU.subtract, ALU.mult).then_inc(done, 1)

            def rotate(i):
                dve.wait_ge(qk_done, i + 1)
                if i == 0:
                    dve.wait_ge(l_rope, 16)
                if i >= 1:
                    dve.wait_ge(qkr_ready, i)
                b = 4 + 2 * (i % 2)
                src = ps[:, b:b + 2, :].rearrange("p b c -> p (b c)")[:, 0:640].rearrange("p (h d) -> p h d", d=HD)
                A = ropeA.rearrange("p (h d) -> p h d", d=HD)
                B = ropeB.rearrange("p (h d) -> p h d", d=HD)
                half = HD // 2

                def table(c, d0, d1):
                    return rope[:, i, c, d0:d1].unsqueeze(1).to_broadcast([P, 20, d1 - d0])

                v.tensor_tensor(A, src, table(0, 0, HD), ALU.mult)
                v.tensor_tensor(B[:, :, 0:half], src[:, :, half:HD], table(1, 0, half), ALU.mult)
                v.tensor_tensor(B[:, :, half:HD], src[:, :, 0:half], table(1, half, HD), ALU.mult)\
                    .then_inc(rope_ready, 1)

            embed(0)
            embed(1)
            normed(0, 0, xn_ready)
            normed(1, 1, xn_ready)
            embed(2)
            embed(3)
            embed(4)
            normed(2, 2, xn_ready)
            rotate(0)
            normed(3, 3, xn_ready)
            rotate(1)
            normed(4, 4, xn_ready)
            rotate(2)
            rotate(3)
            rotate(4)

            def row_max(a, n):
                w, u = AW[a], 4 * a + n
                dve.wait_ge(s_done, u + 1)
                v.tensor_reduce(nmax[0:w, n, :], ps[0:w, n, 0:NGRP * w].rearrange("p (g t) -> p g t", g=NGRP),
                                AX.X, ALU.max, negate=True).then_inc(max_done, 1)

            def recip(a, n):
                w, u = AW[a], 4 * a + n
                dve.wait_ge(exp_done, u + 1)
                v.reciprocal(rden[0:w, n, :], esum[0:w, n, :]).then_inc(rden_ready, 1)

            def prob_T(a, n):
                w, u = AW[a], 4 * a + n
                dve.wait_ge(pT_ps, u + 1)
                if u >= 2:
                    dve.wait_ge(pv_done, u - 1)
                v.tensor_copy(PT[n % 2][0:w, 0:NGRP * w], ps[0:w, 4 + n % 2, 0:NGRP * w]).then_inc(pT_ready, 1)

            def residual(i):
                dve.wait_ge(wo_done, i + 1)
                link(v.tensor_tensor(hres[:, i, :], ps[:, 7, :], hres[:, i, :], ALU.add))
                mean_var(i)

            for a in range(AT + 1):
                for n in range(NKV):
                    if a < AT:
                        row_max(a, n)
                    if a >= 1:
                        prob_T(a - 1, n)
                    if a < AT and n > 0:
                        recip(a, n - 1)
                if a < AT:
                    recip(a, NKV - 1)
                if a >= 3:
                    residual(a - 3)
                    normed(a - 3, TT + a - 3, xn2_ready)
            residual(4)
            normed(4, TT + 4, xn2_ready)

            def grid(x):
                return x.rearrange("p (i e) -> p i e", e=E)

            def over_experts(x):
                return x.unsqueeze(2).to_broadcast([P, TT, E])

            def over_tiles(x):
                return x.unsqueeze(1).to_broadcast([P, TT, E])

            dve.wait_ge(sig_done, 1)
            link(v.tensor_tensor(grid(sbias), grid(sc), over_tiles(gb[:]), ALU.add))
            for sel, m, r in ((sel1, m1, r1), (sel2, m2, r2)):
                link(v.tensor_reduce(m, grid(sbias), AX.X, ALU.max))
                link(v.tensor_tensor(grid(t0), grid(sbias), over_experts(m), ALU.is_equal))
                link(v.tensor_tensor(grid(t0), grid(t0), over_tiles(rev), ALU.mult))
                link(v.tensor_reduce(r, grid(t0), AX.X, ALU.max))
                link(v.tensor_tensor(grid(sel), over_tiles(rev), over_experts(r), ALU.is_equal))
                if sel is sel1:
                    link(v.scalar_tensor_tensor(out=sbias, in0=sel1, scalar=NEG, in1=sbias, op0=ALU.mult, op1=ALU.add))
            v.tensor_tensor(msel, sel1, sel2, ALU.add).then_inc(sel_ready, 1)

            def hidden(j, par):
                dve.wait_ge(u_done, j + 1)
                dve.wait_ge(silu_done, j + 1)
                v.tensor_tensor(hg[:, par, :], ps[:, 2 * par + 1, 0:H], hg[:, par, :], ALU.mult).then_inc(h_done, 1)

            def shared_y(i, u):
                dve.wait_ge(y_done, u + 1)
                v.tensor_tensor(hres[:, i, :], ps[:, 5, :], hres[:, i, :], ALU.add).then_inc(y_used, 1)

            def expert_y(b):
                dve.wait_ge(y_done, b + (EARLY + 1))
                if not isinstance(b, int) or b > 0:
                    dve.wait_ge(y_stored, b * 16)
                v.tensor_copy(yb[:], ps[:, 5, :]).then_inc(y_used, 1)

            hidden(0, 0)
            for t, sel, c in ((t0, sel1, 0), (t1, sel2, 1)):
                link(v.tensor_tensor(t, sc, sel, ALU.mult))
                link(v.tensor_reduce(wtop[:, c, :], grid(t), AX.X, ALU.add))
            link(v.tensor_tensor(wsum, wtop[:, 0, :], wtop[:, 1, :], ALU.add))
            link(v.reciprocal(wsum, wsum))
            link(v.tensor_tensor(wtop[:], wtop[:], wsum.unsqueeze(1).to_broadcast([P, 2, TT]), ALU.mult))
            dve.wait_ge(rank_done, 1)
            tot = ps[:, 7, TT * E:2 * TT * E]
            link(v.tensor_reduce(cnt, tot.rearrange("p (i e) -> p e i", e=E), AX.X, ALU.add))
            ov = over.rearrange("p (e i) -> p e i", i=TT)
            link(v.tensor_tensor(ov, cnt.unsqueeze(2).to_broadcast([P, E, TT]),
                                 thr.unsqueeze(1).to_broadcast([P, E, TT]), ALU.is_gt))
            link(v.tensor_reduce(nblk, ov, AX.X, ALU.add))
            link(v.tensor_tensor_scan(incl, cst[:, C_ONE:C_ONE + E], nblk, 0.0, ALU.mult, ALU.add))
            link(v.tensor_tensor(base0, incl, nblk, ALU.subtract))
            bt = grid(baseT)
            link(v.tensor_scalar(bt[:, 0, :], base0, float(P), None, ALU.mult))
            for i in range(1, TT):
                link(v.tensor_tensor(bt[:, i, :], bt[:, i - 1, :], grid(tot)[:, i - 1, :], ALU.add))
            link(v.tensor_tensor(pos, ps[:, 7, 0:TT * E], baseT, ALU.add))
            for t, sel, c in ((t0, sel1, 0), (t1, sel2, 1)):
                link(v.tensor_tensor(t, pos, sel, ALU.mult))
                link(v.tensor_reduce(slotf[:, c * TT:(c + 1) * TT], grid(t), AX.X, ALU.add))
            v.tensor_copy(slot_i[:].rearrange("p c i -> p (c i)"), slotf).then_inc(slot_ready, 1)
            bc = blkc.rearrange("p (b e) -> p b e", e=E)[0:1]
            link(v.tensor_tensor(bc, incl[0:1].unsqueeze(1).to_broadcast([1, NB, E]),
                                 blki[0:1].unsqueeze(2).to_broadcast([1, NB, E]), ALU.is_le))
            link(v.tensor_reduce(blkf[0:1], bc, AX.X, ALU.add))
            v.tensor_scalar(blk[:], blkf[0:1], float(E - 1), None, ALU.min).then_inc(blk_ready, 1)

            for j in range(1, J0):
                hidden(j, j % 2)
                if j % SH == 0:
                    shared_y(j // SH - 1, j // SH - 1)
            hidden(J0, 0)
            shared_y(EARLY - 1, EARLY - 1)
            with dve.Fori(1, NB, 2) as b:
                for u in range(2):
                    hidden(b + (u + J0), (1 + u) % 2)
                    expert_y(b + (u - 1))
            hidden(J1, J1 % 2)
            expert_y(NB - 1)
            hidden(J1 + 1, (J1 + 1) % 2)

            def combine(i):
                dve.wait_ge(gathered, 2 * TT * 16)
                for c in range(2):
                    link(v.scalar_tensor_tensor(out=hres[:, i, :], in0=yg[:, c, i, :], scalar=wtop[:, c, i:i + 1],
                                                in1=hres[:, i, :], op0=ALU.mult, op1=ALU.add))

            hidden(J1 + 2, (J1 + 2) % 2)
            shared_y(EARLY, EARLY + NB)
            hidden(J1 + 3, (J1 + 3) % 2)
            for i in range(TT):
                dve.wait_ge(y_used, min(i + 1, EARLY) if i < EARLY else EARLY + NB + 1)
                combine(i)
                if i < TT - 1:
                    v.engine_nop().then_inc(out_ready, 1)
            shared_y(TT - 1, EARLY + NB + 1)
            dve.wait_ge(y_used, EARLY + NB + 2)
            v.engine_nop().then_inc(out_ready, 1)

        @block.gpsimd
        def _(pool):
            g = nc.gpsimd
            steps = [0]
            g.memset(halfneg[:], -0.5).then_inc(const_ready, 1)
            g.memset(xb[:], 0.0).then_inc(zero_ready, 1)
            pool.wait_ge(const_ready, 1)

            def inv_std(i, nth):
                pool.wait_ge(stats_ready, nth + 1)
                g.tensor_scalar(rstd[:, i:i + 1], mv[:, i, 1:2], EPS, None, ALU.add).then_inc(pool_step, 1)
                steps[0] += 1
                pool.wait_ge(pool_step, steps[0])
                g.tensor_tensor(rstd[:, i:i + 1], rstd[:, i:i + 1], halfneg[:], ALU.pow).then_inc(rstd_ready, 1)

            def rotate(i):
                pool.wait_ge(rope_ready, i + 1)
                if i >= 2:
                    pool.wait_ge(ropeT_ps, i - 1)
                g.tensor_tensor(qkr[i % 2], ropeA, ropeB, ALU.add).then_inc(qkr_ready, 1)

            for i in range(TT):
                inv_std(i, i)
            for i in range(TT):
                rotate(i)

            def normalise(a, n):
                w, u = AW[a], 4 * a + n
                pool.wait_ge(rden_ready, u + 1)
                p = prob[0:w, n, 0:NGRP * w].rearrange("p (g t) -> p g t", g=NGRP)
                g.tensor_tensor(p, p, rden[0:w, n, :].unsqueeze(2).to_broadcast([w, NGRP, w]), ALU.mult)\
                    .then_inc(prob_ready, 1)

            for a in range(AT):
                for n in range(NKV):
                    normalise(a, n)
                if a >= 3:
                    inv_std(a - 3, TT + a - 3)
            inv_std(3, TT + 3)
            inv_std(4, TT + 4)

            pool.wait_ge(zeroed, 16)
            pool.wait_ge(slot_ready, 1)
            for c in range(2):
                for i in range(TT):
                    g.indirect_dma_start(out=x_disp, out_offset=bass.IndirectOffsetOnAxis(
                        ap=slot_i[:, c, i:i + 1].bitcast(U32), axis=0), in_=xn[:, i, :], in_offset=None)\
                        .then_inc(scattered, 16)
            pool.wait_ge(y_stored, NB * 16)
            pool.wait_ge(y_done, EARLY + NB)
            for i in range(TT):
                for c in range(2):
                    g.indirect_dma_start(out=yg[:, c, i, :], out_offset=None, in_=y_disp,
                                         in_offset=bass.IndirectOffsetOnAxis(
                                             ap=slot_i[:, c, i:i + 1].bitcast(U32), axis=0)).then_inc(gathered, 16)


def constants():
    c = np.zeros((P, C_END), np.float32)
    i = np.arange(P)
    c[:, C_ID:C_ID + P] = i[:, None] == i[None, :]
    c[:, C_TRI:C_TRI + P] = i[:, None] < i[None, :]
    c[:, C_ONE:C_ONE + P] = 1.0
    w = np.arange(WMAX)
    c[:WMAX, C_MASK:C_MASK + WMAX] = np.where(w[:, None] // NPOS == w[None, :] // NPOS, 0.0, NEG)
    c[:, C_REV:C_REV + E] = E - np.arange(E)
    c[:, C_THR:C_THR + TT] = P * np.arange(TT)
    c[:, C_BLK:C_BLK + NB] = np.arange(NB)
    freqs = (1.0 / THETA ** (np.arange(0, HD, 2, dtype=np.float32) / HD)).astype(np.float32)
    emb = np.outer(np.arange(NPOS, dtype=np.float32), freqs).astype(np.float32)
    cos, sin = np.cos(emb), np.sin(emb)
    root = float(HD) ** -0.25
    table = np.stack([np.concatenate([cos, cos], 1), np.concatenate([-sin, sin], 1)], 1) * root
    rows = table[np.arange(TOK) % NPOS].reshape(TT, P, 2 * HD)
    c[:, C_ROPE:C_END] = rows.transpose(1, 0, 2).reshape(P, TT * 2 * HD)
    return c


def kernel(x, L0_tok_W, L0_tok_b, L0_attn_Wq, L0_attn_Wk, L0_attn_Wv, L0_attn_Wo, L0_ffn_gate_w,
           L0_ffn_gate_bias, L0_ffn_shared_gw, L0_ffn_shared_dw, L0_ffn_up_w, L0_ffn_down_w):
    import concourse.bacc as bacc
    from concourse.bass_utils import run_bass_kernel_spmd

    a = {n: np.asarray(v) for n, v in dict(
        x=x, tw=L0_tok_W, tb=L0_tok_b, wq=L0_attn_Wq, wk=L0_attn_Wk, wv=L0_attn_Wv, wo=L0_attn_Wo,
        gw=L0_ffn_gate_w, gb=L0_ffn_gate_bias, sg=L0_ffn_shared_gw, sd=L0_ffn_shared_dw, up=L0_ffn_up_w,
        dn=L0_ffn_down_w).items()}

    def chunks(m):
        return m.reshape(-1, P, m.shape[1]).transpose(1, 0, 2)

    wq = a["wq"].reshape(D, NKV, NGRP, HD).transpose(0, 2, 1, 3).reshape(D, D)
    wqkv = chunks(np.concatenate([wq, a["wk"], a["wv"]], 1))
    wo = a["wo"].reshape(NKV, NGRP, HD, D).transpose(0, 2, 1, 3).reshape(P, NGRP, D)
    ups = [np.concatenate([a["sg"][(SH + s) * H:(SH + s + 1) * H], a["sg"][s * H:(s + 1) * H]]) for s in range(SH)]
    dns = [a["sd"][:, s * H:(s + 1) * H] for s in range(SH)]
    ups += [a["up"][e] for e in range(E)]
    dns += [a["dn"][e] for e in range(E)]
    wa = np.stack([np.concatenate([chunks(u.T).reshape(P, UPW), chunks(d.T[:2 * P]).reshape(P, 2 * D)], 1)
                   for u, d in zip(ups, dns)])
    wb = np.stack([d.T[2 * P:] for d in dns])
    ins = [("xT", a["x"][:, :, 0].T), ("tok_w", a["tw"].T), ("tok_b", a["tb"]), ("consts", constants()),
           ("wqkv", wqkv), ("wo", wo), ("gate_w", chunks(a["gw"].T)), ("gate_b", a["gb"]), ("wa", wa), ("wb", wb)]

    nc = bacc.Bacc("TRN2", target_bir_lowering=False, num_devices=1)
    arrays, args = {}, []
    for name, v in ins:
        v = np.ascontiguousarray(v)
        arrays[name + "_in"] = v
        args.append(nc.dram_tensor(name + "_in", v.shape, mybir.dt.from_np(v.dtype), kind="ExternalInput").ap())
    out = nc.dram_tensor("out_0", (BATCH, NPOS, D), F32, kind="ExternalOutput").ap()
    build(nc, *args, out)
    r = run_bass_kernel_spmd(nc, [arrays], core_ids=[0])
    return r.results[0]["out_0"]
```

```python
from contextlib import ExitStack

import numpy as np

import concourse.bass as bass
from concourse import mybir
from concourse.alu_op_type import AluOpType as ALU

F32 = mybir.dt.float32
BF16 = mybir.dt.bfloat16
I32 = mybir.dt.int32
U32 = mybir.dt.uint32
ACT = mybir.ActivationFunctionType
AX = mybir.AxisListType

P = 128
BATCH, SEQ = 64, 750
PATCH, STRIDE = 128, 64
NPOS = (SEQ - PATCH) // STRIDE + 1
TOK = BATCH * NPOS
D = 512
KC = D // P
TT = TOK // P
NKV, NGRP, HD = 4, 4, 32
THETA = 10000.0
EPS = 1e-5

GB = 3
GQ = GB * NPOS
GK = 32
NG = -(-BATCH // GB)
TG = 4
AT = -(-NG // TG)
AG = [min(TG, NG - TG * a) for a in range(AT)]
TOKP = NG * GQ + GK
QROWS = NGRP * GQ
NEG = -1e30

E = 8
H = 352
SH = 2
HC = [P, P, H - 2 * P]
UPW = KC * 2 * H
WA = UPW + 2 * D
SLOT = UPW + 3 * D
NSLOT = SH + E
NB = (2 * TOK + E * (P - 1)) // P
EARLY = 3
J0 = SH * EARLY
LATE = SH * (TT - EARLY)
TMIN = 2 * TOK // P + 1
FIRST_FRONT = 5

C_ID, C_TRI, C_ONE, C_MASK = 0, P, 2 * P, 3 * P
C_REV = C_MASK + GK
C_THR = C_REV + E
C_BLK = C_THR + TT
C_HEAD = C_BLK + NB + 1
C_ROPE = C_HEAD + NKV
C_END = C_ROPE + TT * 2 * HD


def build(nc, xT, tok_w, tok_b, consts, wqkv, wo, gate_w, gate_b, wa, wb, out):
    x_disp = nc.dram_tensor("x_disp", [(NB + 1) * P, D], F32, kind="Internal").ap()
    y_disp = nc.dram_tensor("y_disp", [NB * P, D], F32, kind="Internal").ap()
    out_rows = out.rearrange("b n d -> (b n) d")

    ctx = ExitStack()
    with ctx:
        def sb(name, shape, dt=F32):
            return ctx.enter_context(nc.sbuf_tensor(name, shape, dt))

        def sem(name):
            return ctx.enter_context(nc.semaphore(name))

        W = sb("weights", [P, NSLOT * SLOT])
        hres = sb("hres", [P, TT, D])
        xn2T = sb("xn2T", [P, KC, TOK])
        xb = sb("xb", [P, D])
        xbT = sb("xbT", [P, 2, KC, P])
        hg = sb("hg", [P, 2, H])
        hT = sb("hT", [P, 3, P])
        yb = sb("yb", [P, D])
        cst = sb("cst", [P, C_ROPE])
        identb = sb("identb", [P, P], BF16)
        maskb = sb("maskb", [P, GK], BF16)
        gw = sb("gw", [P, KC, E])
        gb = sb("gb", [P, E])
        halfneg = sb("halfneg", [P, 1])
        stats = sb("stats", [P, 2, 6])
        mv = sb("mv", [P, TT, 2])
        rstd = sb("rstd", [P, TT])
        nmax = sb("nmax", [P, 2, TG * NKV])
        esum = sb("esum", [P, 2, TG * NKV])
        rden = sb("rden", [P, 2, TG * NKV])
        slot_i = sb("slot_i", [P, 2, TT], I32)
        wtop = sb("wtop", [P, 2, TT])
        blk = sb("blk", [1, NB + 1], I32)
        trip = sb("trip", [1, 1], I32)
        ps = ctx.enter_context(nc.psum_tensor("ps", [P, 8, 512], F32))

        ident = cst[:, C_ID:C_ID + P]
        tri = cst[:, C_TRI:C_TRI + P]
        ones = cst[:, C_ONE:C_ONE + P]
        rev = cst[:, C_REV:C_REV + E]
        thr = cst[:, C_THR:C_THR + TT]
        blki = cst[:, C_BLK:C_BLK + NB + 1]
        headm = cst[:, C_HEAD:C_HEAD + NKV]

        at = [FIRST_FRONT * SLOT]

        def front(n):
            at[0] += n
            return W[:, at[0] - n:at[0]]

        praw = front(NPOS * BATCH)
        pT = front(TOK)
        ropeA, ropeB = praw, pT
        tokw = front(D)
        tokb = front(D)
        rope = front(TT * 2 * HD).rearrange("p (i c d) -> p i c d", i=TT, c=2)
        wqkv_sb = front(KC * 768).rearrange("p (k n) -> p k n", k=KC)
        wo_sb = front(NGRP * D).rearrange("p (g n) -> p g n", g=NGRP)
        qkr = [front(640) for _ in range(2)]
        xnT = front(KC * TOKP).rearrange("p (k t) -> p k t", k=KC)
        yT = xnT
        QT = front(NGRP * TOKP)
        KT = front(TOKP)
        VT = front(TOKP)
        PT = [front(TG * QROWS) for _ in range(2)]
        wide = wqkv_sb.rearrange("p k n -> p (k n)")
        KD, VD, VB = ([wide[:, (2 * c + u) * 512:(2 * c + u + 1) * 512] for u in range(2)] for c in range(3))
        assert at[0] <= (NSLOT - 1) * SLOT
        at[0] = (NSLOT - 1) * SLOT
        xn = front(TT * D).rearrange("p (i d) -> p i d", i=TT)
        prob_at = at[0]
        prob = [front(TG * P) for _ in range(2)]
        assert at[0] <= NSLOT * SLOT
        at[0] = prob_at

        def routing(n):
            return front(n)

        sc, sbias, t0, t1, sel1, sel2, msel, pos = (routing(TT * E) for _ in range(8))
        m1, m2, r1, r2, wsum = (routing(TT) for _ in range(5))
        cnt, nblk, incl, base0 = (routing(E) for _ in range(4))
        over = routing(E * TT)
        baseT = routing(TT * E)
        blkc = routing((NB + 1) * E)
        blkf = routing(NB + 1)
        tripc = routing(E)
        slotf = routing(2 * TT)
        assert at[0] <= NSLOT * SLOT
        yg = W[:, SH * SLOT:SH * SLOT + 2 * TT * D].rearrange("p (c i d) -> p c i d", c=2, i=TT)

        l_x, l_tokw, l_tokb, l_cst, l_rope = (sem(n) for n in ("l_x", "l_tokw", "l_tokb", "l_cst", "l_rope"))
        l_qkv, l_wo, l_gate = sem("l_qkv"), sem("l_wo"), sem("l_gate")
        l_slot = [sem(f"l_slot{s}") for s in range(NSLOT)]
        zeroed, scattered, xb_loaded = sem("zeroed"), sem("scattered"), sem("xb_loaded")
        all_stored = sem("all_stored")
        y_stored, gathered, out_stored = sem("y_stored"), sem("gathered"), sem("out_stored")
        (tok_done, xnT_ps, qk_done, vT_ps, ropeT_ps, s_done, vB_ps, pT_ps, pv_done, wo_done, x2T_ps,
         logit_done, rank_done, xbT_ps) = (sem(n) for n in (
             "tok_done", "xnT_ps", "qk_done", "vT_ps", "ropeT_ps", "s_done", "vB_ps", "pT_ps", "pv_done", "wo_done",
             "x2T_ps", "logit_done", "rank_done", "xbT_ps"))
        (bf_ready, xnT_ready, qkT_ready, vT_ready, exp_done, yT_ready, x2T_ready, sig_done, xbT_ready) = (
            sem(n) for n in ("bf_ready", "xnT_ready", "qkT_ready", "vT_ready", "exp_done", "yT_ready", "x2T_ready",
                             "sig_done", "xbT_ready"))
        (patch_ready, tok_used, stats_ready, xn_ready, rope_ready, kd_ready, vb_ready, sub_done, rden_ready, pT_ready,
         resid_done, xn2_ready, sel_ready, slot_ready, blk_ready, out_ready, dve_step) = (sem(n) for n in (
             "patch_ready", "tok_used", "stats_ready", "xn_ready", "rope_ready", "kd_ready", "vb_ready", "sub_done",
             "rden_ready", "pT_ready", "resid_done", "xn2_ready", "sel_ready", "slot_ready", "blk_ready", "out_ready", "dve_step"))
        const_ready, zero_ready, pad_ready, rstd_ready, qkr_ready, vd_ready, prob_ready, pool_step = (sem(n) for n in (
            "const_ready", "zero_ready", "pad_ready", "rstd_ready", "qkr_ready", "vd_ready", "prob_ready", "pool_step"))

        def pair(name):
            return [sem(name), sem("late_" + name)]

        g_done, u_done, hT_ps, y_done = pair("g_done"), pair("u_done"), pair("hT_ps"), pair("y_done")
        silu_done, hT_ready = pair("silu_done"), pair("hT_ready")
        h_done, y_used = pair("h_done"), pair("y_used")

        def up(s, k, half):
            o = s * SLOT + k * 2 * H + half * H
            return W[:, o:o + H]

        def down(s, c):
            o = s * SLOT + UPW + c * D
            return W[0:HC[c], o:o + D]

        block = ctx.enter_context(nc.Block())

        @block.sync
        def _(sp):
            sp.dma_start(praw.rearrange("p (n b) -> p n b", n=NPOS),
                         bass.AP(xT.tensor, 0, [[BATCH, P], [STRIDE * BATCH, NPOS], [1, BATCH]])).then_inc(l_x, 16)
            sp.dma_start(tokw, tok_w).then_inc(l_tokw, 16)
            sp.dma_start(tokb, bass.AP(tok_b.tensor, 0, [[0, P], [1, D]])).then_inc(l_tokb, 16)
            sp.dma_start(wqkv_sb, wqkv).then_inc(l_qkv, 16)
            sp.dma_start(wo_sb, wo).then_inc(l_wo, 16)
            sp.dma_start(gw[:], gate_w).then_inc(l_gate, 16)
            sp.dma_start(gb[:], bass.AP(gate_b.tensor, 0, [[0, P], [1, E]])).then_inc(l_gate, 16)

            def load_slot(s):
                sp.dma_start(W[:, s * SLOT:s * SLOT + WA], wa[s]).then_inc(l_slot[s], 16)
                sp.dma_start(W[0:HC[2], s * SLOT + WA:(s + 1) * SLOT], wb[s]).then_inc(l_slot[s], 16)

            for s in range(FIRST_FRONT):
                load_slot(s)
            sp.wait_ge(zero_ready, 1)
            sp.dma_start(x_disp.rearrange("(b p) d -> p b d", p=P),
                         bass.AP(xb, 0, [[D, P], [0, NB + 1], [1, D]])).then_inc(zeroed, 16)
            sp.dma_start(y_disp[TMIN * P:, :].rearrange("(b p) d -> p b d", p=P),
                         bass.AP(xb, 0, [[D, P], [0, NB - TMIN], [1, D]])).then_inc(zeroed, 16)
            sp.wait_ge(wo_done, TT)
            for s in range(FIRST_FRONT, NSLOT - 1):
                load_slot(s)
            sp.wait_ge(scattered, 2 * TT * 16)
            sp.wait_ge(blk_ready, 1)
            sp.dma_start(xb[:], x_disp[0:P, :]).then_inc(xb_loaded, 16)
            load_slot(NSLOT - 1)
            last_b = sp.value_load(trip[0:1, 0:1], min_val=TMIN - 1, max_val=NB - 1)

            def load_x(b):
                sp.wait_ge(xbT_ps, b)
                sp.dma_start(xb[:], x_disp[bass.ds(b * P, P), :]).then_inc(xb_loaded, 16)

            def store_y(b):
                sp.wait_ge(y_used[0], b + (EARLY + 1))
                sp.dma_start(y_disp[bass.ds(b * P, P), :], yb[:]).then_inc(y_stored, 16)

            load_x(1)
            load_x(2)
            with sp.Fori(3, last_b + 2) as b:
                load_x(b)
                store_y(b - 3)
            store_y(last_b - 1)
            store_y(last_b)
            sp.wait_ge(y_stored, last_b * 16 + 16)
            sp.sem_inc(all_stored, 1)
            for i in range(TT):
                sp.wait_ge(out_ready, i + 1)
                sp.dma_start(out_rows[i * P:(i + 1) * P, :], hres[:, i, :]).then_inc(out_stored, 16)
            sp.wait_ge(out_stored, TT * 16)

        @block.tensor
        def _(pe):
            mm = nc.tensor.matmul

            def transposes(dst, srcs, ident_ap):
                for o, src in zip(dst, srcs):
                    last = nc.tensor.transpose(o, src, ident_ap)
                return last

            pe.wait_ge(patch_ready, 1)
            pe.wait_ge(l_tokw, 16)
            for i in range(TT):
                if i >= 2:
                    pe.wait_ge(tok_used, i - 1)
                mm(ps[:, i % 2, :], pT[:, i * P:(i + 1) * P], tokw, start=True, stop=True).then_inc(tok_done, 1)

            def norm_T(i):
                pe.wait_ge(xn_ready, i + 1)
                pe.wait_ge(l_cst, 16)
                if i >= 2:
                    pe.wait_ge(xnT_ready, i - 1)
                b = 2 + i % 2
                transposes([ps[:, b, k * P:(k + 1) * P] for k in range(KC)],
                           [xn[:, i, k * P:(k + 1) * P] for k in range(KC)], ident).then_inc(xnT_ps, 1)

            def project(i):
                pe.wait_ge(xnT_ready, i + 1)
                pe.wait_ge(l_qkv, 16)
                if i >= 2:
                    pe.wait_ge(qkT_ready, i - 1)
                b = 4 + 2 * (i % 2)
                for c, n0, n1 in ((0, 0, 512), (1, 512, 640)):
                    for k in range(KC):
                        last = mm(ps[:, b + c, 0:n1 - n0], xnT[:, k, i * P:(i + 1) * P], wqkv_sb[:, k, n0:n1],
                                  start=(k == 0), stop=(k == KC - 1))
                last.then_inc(qk_done, 1)

            def rope_T(i):
                pe.wait_ge(qkr_ready, i + 1)
                b = 4 + 2 * (i % 2)
                r = qkr[i % 2]
                transposes([ps[:, b + c // 4, (c % 4) * P:(c % 4 + 1) * P] for c in range(5)],
                           [r[:, c * P:(c + 1) * P] for c in range(5)], ident).then_inc(ropeT_ps, 1)

            def values(i):
                pe.wait_ge(tok_used, TT) if i < 2 else pe.wait_ge(vT_ready, i - 1)
                for k in range(KC):
                    last = mm(ps[:, i % 2, 0:P], wqkv_sb[:, k, 640:768], xnT[:, k, i * P:(i + 1) * P],
                              start=(k == 0), stop=(k == KC - 1))
                last.then_inc(vT_ps, 1)

            norm_T(0)
            project(0)
            norm_T(1)
            project(1)
            for i in range(TT):
                rope_T(i)
                values(i)
                if i + 2 < TT:
                    norm_T(i + 2)
                    project(i + 2)

            def scores(a):
                n = AG[a] * P
                pe.wait_ge(sub_done, a - 1) if a >= 2 else pe.wait_ge(vT_ready, TT)
                mm(ps[0:QROWS, a % 2, 0:n], identb[0:QROWS, 0:QROWS],
                   maskb[0:QROWS, :].unsqueeze(1).to_broadcast([QROWS, AG[a] * NKV, GK]), start=True, stop=False)
                pe.wait_ge(kd_ready, a + 1)
                for j in range(AG[a]):
                    t = (TG * a + j) * GQ
                    last = mm(ps[0:QROWS, a % 2, j * P:(j + 1) * P], QT[:, t * NGRP:(t + GQ) * NGRP], KD[a % 2][:, j * P:(j + 1) * P],
                              start=False, stop=(j == AG[a] - 1))
                last.then_inc(s_done, 1)

            def value_blocks(a):
                pe.wait_ge(vd_ready, a + 1)
                if a >= 1:
                    pe.wait_ge(vb_ready, a)
                transposes([ps[:, 2, j * P:(j + 1) * P] for j in range(AG[a])],
                           [VD[a % 2][:, j * P:(j + 1) * P] for j in range(AG[a])], ident).then_inc(vB_ps, 1)

            def prob_T(a):
                pe.wait_ge(prob_ready, a + 1)
                if a >= 2:
                    pe.wait_ge(pT_ready, a - 1)
                transposes([ps[:, 4 + a % 2, j * QROWS:(j + 1) * QROWS] for j in range(AG[a])],
                           [prob[a % 2][0:QROWS, j * P:(j + 1) * P] for j in range(AG[a])],
                           ident[0:QROWS, 0:QROWS]).then_inc(pT_ps, 1)

            def prob_v(a):
                pe.wait_ge(pT_ready, a + 1)
                pe.wait_ge(vb_ready, a + 1)
                if a >= 1:
                    pe.wait_ge(yT_ready, a)
                for j in range(AG[a]):
                    c = slice(j * QROWS, (j + 1) * QROWS)
                    last = mm(ps[:, 6, c], VB[a % 2][:, j * P:(j + 1) * P], PT[a % 2][:, c], start=True, stop=True)
                last.then_inc(pv_done, 1)

            def out_proj(i):
                pe.wait_ge(yT_ready, min(i + 2, AT))
                pe.wait_ge(l_wo, 16)
                pe.wait_ge(resid_done, i) if i >= 1 else pe.wait_ge(xnT_ready, TT)
                for g in range(NGRP):
                    last = mm(ps[:, 3, :], yT[:, g, i * P:(i + 1) * P], wo_sb[:, g, :],
                              start=(g == 0), stop=(g == NGRP - 1))
                last.then_inc(wo_done, 1)

            def norm2_T(i):
                pe.wait_ge(xn2_ready, i + 1)
                if i >= 1:
                    pe.wait_ge(x2T_ready, i)
                transposes([ps[:, 7, k * P:(k + 1) * P] for k in range(KC)],
                           [xn[:, i, k * P:(k + 1) * P] for k in range(KC)], ident).then_inc(x2T_ps, 1)

            pe.wait_ge(bf_ready, 1)
            pe.wait_ge(xnT_ready, TT)
            pe.wait_ge(qkT_ready, TT)
            for a in range(2):
                scores(a)
                value_blocks(a)
            for a in range(AT):
                prob_T(a)
                if a + 2 < AT:
                    scores(a + 2)
                if a >= 2:
                    out_proj(a - 2)
                prob_v(a)
                if a + 2 < AT:
                    value_blocks(a + 2)
                if a >= 3:
                    norm2_T(a - 3)
            out_proj(TT - 1)
            norm2_T(TT - 2)

            def logits():
                pe.wait_ge(l_gate, 32)
                pe.wait_ge(yT_ready, AT)
                pe.wait_ge(x2T_ready, TT)
                for i in range(TT):
                    for k in range(KC):
                        last = mm(ps[:, 6, i * E:(i + 1) * E], xn2T[:, k, i * P:(i + 1) * P], gw[:, k, :],
                                  start=(k == 0), stop=(k == KC - 1))
                last.then_inc(logit_done, 1)

            def ranks():
                pe.wait_ge(sel_ready, 1)
                mm(ps[:, 7, 0:TT * E], tri, msel, start=True, stop=True)
                mm(ps[:, 7, TT * E:2 * TT * E], ones, msel, start=True, stop=True).then_inc(rank_done, 1)

            def gate_up(ph, par, half, xk, w):
                for k in range(KC):
                    last = mm(ps[:, 2 * par + half, 0:H], xk(k), w(k, half), start=(k == 0), stop=(k == KC - 1))
                last.then_inc((u_done if half else g_done)[ph], 1)

            def hidden_T(ph, j, par):
                pe.wait_ge(h_done[ph], j + 1)
                for c in range(3):
                    last = nc.tensor.transpose(ps[0:HC[c], 4, c * P:(c + 1) * P], hg[:, par, c * P:c * P + HC[c]], ident)
                last.then_inc(hT_ps[ph], 1)

            def down_proj(ph, j, w, first=True, final=True):
                pe.wait_ge(hT_ready[ph], j + 1)
                for c in range(3):
                    last = mm(ps[:, 5, :], hT[0:HC[c], c, :], w(c), start=(first and c == 0), stop=(final and c == 2))
                if final:
                    last.then_inc(y_done[ph], 1)

            def block_T(b):
                pe.wait_ge(xb_loaded, (b + 1) * 16)
                transposes([ps[:, 7, k * P:(k + 1) * P] for k in range(KC)],
                           [xb[:, k * P:(k + 1) * P] for k in range(KC)], ident).then_inc(xbT_ps, 1)

            def shared_gate_up(ph, j, half):
                i = j // SH + EARLY * ph
                gate_up(ph, (j + ph) % 2, half, lambda k: xn2T[:, k, i * P:(i + 1) * P],
                        lambda k, h: up(j % SH, k, h))

            def shared_down(ph, j):
                if j % SH == 0 and j > 0:
                    pe.wait_ge(y_used[ph], j // SH)
                down_proj(ph, j, lambda c: down(j % SH, c), first=(j % SH == 0), final=(j % SH == SH - 1))

            pe.wait_ge(sub_done, AT)
            pe.wait_ge(vb_ready, AT)
            for j in range(J0):
                if j < SH:
                    pe.wait_ge(l_slot[j], 32)
                if j == 0:
                    pe.wait_ge(x2T_ready, 1)
                if j == 1:
                    pe.wait_ge(resid_done, TT)
                shared_gate_up(0, j, 0)
                if j > 0:
                    hidden_T(0, j - 1, (j - 1) % 2)
                shared_gate_up(0, j, 1)
                if j == 0:
                    norm2_T(TT - 1)
                    pe.wait_ge(pT_ready, AT)
                if j > 0:
                    shared_down(0, j - 1)
                if j == 1:
                    logits()
                if j == 2:
                    ranks()

            def expert_of(b):
                return pe.value_load(blk[0:1, b:b + 1] if isinstance(b, int) else blk[0:1, bass.ds(b, 1)],
                                     min_val=0, max_val=E - 1)

            def expert_up(e):
                return lambda k, half: W[:, bass.ds(e * SLOT + (SH * SLOT + k * 2 * H + half * H), H)]

            def expert_down(e):
                return lambda c: W[0:HC[c], bass.ds(e * SLOT + (SH * SLOT + UPW + c * D), D)]

            def expert_step(b, par, before):
                e = expert_of(b)
                pe.wait_ge(xbT_ready, b + 1)
                gate_up(0, par, 0, lambda k: xbT[:, par, k, :], expert_up(e))
                hidden_T(0, b + (J0 - 1), 1 - par)
                block_T(b + 1)
                gate_up(0, par, 1, lambda k: xbT[:, par, k, :], expert_up(e))
                before()

            def expert_tail(b):
                w = expert_down(expert_of(b))
                pe.wait_ge(y_used[0], b + EARLY)
                down_proj(0, b + J0, w)

            pe.wait_ge(slot_ready, 1)
            block_T(0)
            pe.wait_ge(blk_ready, 1)
            for s in range(SH, NSLOT):
                pe.wait_ge(l_slot[s], 32)
            expert_step(0, 0, lambda: shared_down(0, J0 - 1))
            last_b = pe.value_load(trip[0:1, 0:1], min_val=TMIN - 1, max_val=NB - 1)
            with pe.Fori(1, last_b + 1, 2) as b:
                for u in range(2):
                    expert_step(b + u, (1 + u) % 2, lambda: expert_tail(b + (u - 1)))

            for j in range(LATE):
                shared_gate_up(1, j, 0)
                if j == 0:
                    hidden_T(0, last_b + J0, 0)
                else:
                    hidden_T(1, j - 1, j % 2)
                shared_gate_up(1, j, 1)
                if j == 0:
                    expert_tail(last_b)
                    pe.wait_ge(y_used[0], last_b + (EARLY + 1))
                else:
                    shared_down(1, j - 1)
            hidden_T(1, LATE - 1, LATE % 2)
            shared_down(1, LATE - 1)

        @block.scalar
        def _(act):
            act.dma_start(cst[:], consts[:, 0:C_ROPE]).then_inc(l_cst, 16)
            act.dma_start(rope, consts[:, C_ROPE:C_END].rearrange("p (i c d) -> p i c d", i=TT, c=2)).then_inc(l_rope, 16)
            copy = nc.scalar.copy
            act.wait_ge(l_cst, 16)
            copy(identb[:], ident)
            copy(maskb[:], cst[:, C_MASK:C_MASK + GK]).then_inc(bf_ready, 1)

            def norm_T(i):
                act.wait_ge(xnT_ps, i + 1)
                copy(xnT[:, :, i * P:(i + 1) * P], ps[:, 2 + i % 2, :].rearrange("p (k t) -> p k t", k=KC))\
                    .then_inc(xnT_ready, 1)

            def rope_T(i):
                act.wait_ge(ropeT_ps, i + 1)
                b = 4 + 2 * (i % 2)
                copy(QT[:, i * P * NGRP:(i + 1) * P * NGRP].rearrange("p (t g) -> p g t", g=NGRP),
                     ps[:, b, :].rearrange("p (g t) -> p g t", g=NGRP))
                copy(KT[:, i * P:(i + 1) * P], ps[:, b + 1, 0:P]).then_inc(qkT_ready, 1)

            def values(i):
                act.wait_ge(vT_ps, i + 1)
                copy(VT[:, i * P:(i + 1) * P], ps[:, i % 2, 0:P]).then_inc(vT_ready, 1)

            norm_T(0)
            norm_T(1)
            for i in range(TT):
                rope_T(i)
                values(i)
                if i + 2 < TT:
                    norm_T(i + 2)

            def exps(a):
                n = AG[a] * P
                act.wait_ge(sub_done, a + 1)
                p = prob[a % 2][0:QROWS, 0:n]
                nc.scalar.activation(p, p, ACT.Exp).then_inc(exp_done, 1)

            def values_out(a):
                act.wait_ge(pv_done, a + 1)
                t = TG * a * GQ
                o = yT[:, :, t:t + AG[a] * GQ]
                copy(o, ps[:, 6, 0:AG[a] * QROWS].rearrange("p (t g) -> p g t", g=NGRP)).then_inc(yT_ready, 1)

            def norm2_T(i):
                act.wait_ge(x2T_ps, i + 1)
                copy(xn2T[:, :, i * P:(i + 1) * P], ps[:, 7, :].rearrange("p (k t) -> p k t", k=KC))\
                    .then_inc(x2T_ready, 1)

            exps(0)
            exps(1)
            for a in range(AT):
                if a + 2 < AT:
                    exps(a + 2)
                values_out(a)
                if a >= 3:
                    norm2_T(a - 3)
            norm2_T(TT - 2)

            def silu(ph, j, par):
                act.wait_ge(g_done[ph], j + 1)
                nc.scalar.activation(hg[:, par, :], ps[:, 2 * par, 0:H], ACT.Silu).then_inc(silu_done[ph], 1)

            def hidden_T(ph, j):
                act.wait_ge(hT_ps[ph], j + 1)
                copy(hT[:, 0:2, :], ps[:, 4, 0:2 * P].rearrange("p (c t) -> p c t", c=2))
                copy(hT[0:HC[2], 2, :], ps[0:HC[2], 4, 2 * P:3 * P]).then_inc(hT_ready[ph], 1)

            def block_T(b, par):
                act.wait_ge(xbT_ps, b + 1)
                copy(xbT[:, par, :, :], ps[:, 7, :].rearrange("p (k t) -> p k t", k=KC)).then_inc(xbT_ready, 1)

            silu(0, 0, 0)
            norm2_T(TT - 1)
            hidden_T(0, 0)
            silu(0, 1, 1)
            act.wait_ge(logit_done, 1)
            nc.scalar.activation(sc, ps[:, 6, 0:TT * E], ACT.Sigmoid).then_inc(sig_done, 1)

            for j in range(2, J0):
                hidden_T(0, j - 1)
                silu(0, j, j % 2)
            block_T(0, 0)
            hidden_T(0, J0 - 1)
            block_T(1, 1)
            silu(0, J0, 0)
            last_b = act.value_load(trip[0:1, 0:1], min_val=TMIN - 1, max_val=NB - 1)
            with act.Fori(1, last_b + 1, 2) as b:
                for u in range(2):
                    hidden_T(0, b + (u + J0 - 1))
                    block_T(b + (u + 1), u % 2)
                    silu(0, b + (u + J0), (1 + u) % 2)
            for j in range(LATE):
                hidden_T(0, last_b + J0) if j == 0 else hidden_T(1, j - 1)
                silu(1, j, (j + 1) % 2)
            hidden_T(1, LATE - 1)

        @block.vector
        def _(dve):
            v = nc.vector
            steps = [0]

            def link(ins):
                steps[0] += 1
                ins.then_inc(dve_step, 1)
                dve.wait_ge(dve_step, steps[0])

            dve.wait_ge(l_x, 16)
            v.tensor_copy(pT.rearrange("p (b n) -> p b n", n=NPOS), praw.rearrange("p (n b) -> p b n", n=NPOS))\
                .then_inc(patch_ready, 1)

            def mean_var(i):
                link(v.bn_stats(stats[:, i % 2, :], hres[:, i, :]))
                v.bn_aggr(mv[:, i, :], stats[:, i % 2, :]).then_inc(stats_ready, 1)

            def embed(i):
                dve.wait_ge(tok_done, i + 1)
                if i == 0:
                    dve.wait_ge(l_tokb, 16)
                v.tensor_tensor(hres[:, i, :], ps[:, i % 2, :], tokb, ALU.add).then_inc(tok_used, 1)
                dve.wait_ge(tok_used, i + 1)
                mean_var(i)

            def normed(i, nth, done):
                dve.wait_ge(rstd_ready, nth + 1)
                v.tensor_scalar(xn[:, i, :], hres[:, i, :], mv[:, i, 0:1], rstd[:, i:i + 1],
                                ALU.subtract, ALU.mult).then_inc(done, 1)

            def rotate(i):
                dve.wait_ge(qk_done, i + 1)
                if i == 0:
                    dve.wait_ge(l_rope, 16)
                if i >= 1:
                    dve.wait_ge(qkr_ready, i)
                b = 4 + 2 * (i % 2)
                src = ps[:, b:b + 2, :].rearrange("p b c -> p (b c)")[:, 0:640].rearrange("p (h d) -> p h d", d=HD)
                A = ropeA.rearrange("p (h d) -> p h d", d=HD)
                B = ropeB.rearrange("p (h d) -> p h d", d=HD)
                half = HD // 2

                def table(c, d0, d1):
                    return rope[:, i, c, d0:d1].unsqueeze(1).to_broadcast([P, 20, d1 - d0])

                v.tensor_tensor(A, src, table(0, 0, HD), ALU.mult)
                v.tensor_tensor(B[:, :, 0:half], src[:, :, half:HD], table(1, 0, half), ALU.mult)
                v.tensor_tensor(B[:, :, half:HD], src[:, :, 0:half], table(1, half, HD), ALU.mult)\
                    .then_inc(rope_ready, 1)

            embed(0)
            embed(1)
            normed(0, 0, xn_ready)
            normed(1, 1, xn_ready)
            embed(2)
            embed(3)
            embed(4)
            normed(2, 2, xn_ready)
            rotate(0)
            normed(3, 3, xn_ready)
            rotate(1)
            normed(4, 4, xn_ready)
            rotate(2)
            rotate(3)
            rotate(4)

            def spread_k(a):
                n, t = AG[a], TG * a * GQ
                if a >= 2:
                    dve.wait_ge(s_done, a - 1)
                src = bass.AP(KT.tensor, KT.offset + t, [list(KT.ap[0]), [GQ, n], [0, NKV], [1, GK]])
                v.tensor_tensor(KD[a % 2][:, 0:n * P].rearrange("p (j n k) -> p j n k", j=n, k=GK), src, head_mask(n),
                                ALU.mult).then_inc(kd_ready, 1)

            def head_mask(n):
                return bass.AP(headm.tensor, headm.offset, [list(headm.ap[0]), [0, n], [1, NKV], [0, GK]])

            def cols(x):
                return x.rearrange("p (c k) -> p c k", k=GK)

            def soft_a(a):
                n = AG[a] * NKV
                dve.wait_ge(s_done, a + 1)
                s = cols(ps[0:QROWS, a % 2, 0:n * GK])
                link(v.tensor_reduce(nmax[0:QROWS, a % 2, 0:n], s, AX.X, ALU.max))
                if a >= 2:
                    dve.wait_ge(pT_ps, a - 1)
                v.tensor_tensor(cols(prob[a % 2][0:QROWS, 0:n * GK]), s,
                                nmax[0:QROWS, a % 2, 0:n].unsqueeze(2).to_broadcast([QROWS, n, GK]),
                                ALU.subtract).then_inc(sub_done, 1)

            def soft_b(a):
                n = AG[a] * NKV
                dve.wait_ge(exp_done, a + 1)
                p = cols(prob[a % 2][0:QROWS, 0:n * GK])
                link(v.tensor_reduce(esum[0:QROWS, a % 2, 0:n], p, AX.X, ALU.add))
                v.reciprocal(rden[0:QROWS, a % 2, 0:n], esum[0:QROWS, a % 2, 0:n]).then_inc(rden_ready, 1)

            def value_blocks(a):
                dve.wait_ge(vB_ps, a + 1)
                if a >= 2:
                    dve.wait_ge(pv_done, a - 1)
                v.tensor_copy(VB[a % 2][:, 0:AG[a] * P], ps[:, 2, 0:AG[a] * P]).then_inc(vb_ready, 1)

            def prob_T(a):
                dve.wait_ge(pT_ps, a + 1)
                if a >= 2:
                    dve.wait_ge(pv_done, a - 1)
                v.tensor_copy(PT[a % 2][:, 0:AG[a] * QROWS], ps[:, 4 + a % 2, 0:AG[a] * QROWS]).then_inc(pT_ready, 1)

            def residual(i):
                dve.wait_ge(wo_done, i + 1)
                v.tensor_tensor(hres[:, i, :], ps[:, 3, :], hres[:, i, :], ALU.add).then_inc(resid_done, 1)
                dve.wait_ge(resid_done, i + 1)
                mean_var(i)

            dve.wait_ge(qkT_ready, TT)
            dve.wait_ge(vT_ps, TT)
            dve.wait_ge(pad_ready, 1)
            spread_k(0)
            spread_k(1)
            for a in range(2):
                soft_a(a)
                value_blocks(a)
                soft_b(a)
            spread_k(2)
            for a in range(AT):
                prob_T(a)
                if a >= 2:
                    residual(a - 2)
                if a + 2 < AT:
                    soft_a(a + 2)
                    if a + 3 < AT:
                        spread_k(a + 3)
                    soft_b(a + 2)
                    value_blocks(a + 2)
                if a >= 2:
                    normed(a - 2, TT + a - 2, xn2_ready)
            residual(TT - 1)
            normed(TT - 1, 2 * TT - 1, xn2_ready)

            def grid(x):
                return x.rearrange("p (i e) -> p i e", e=E)

            def over_experts(x):
                return x.unsqueeze(2).to_broadcast([P, TT, E])

            def over_tiles(x):
                return x.unsqueeze(1).to_broadcast([P, TT, E])

            def hidden(ph, j, par):
                dve.wait_ge(u_done[ph], j + 1)
                dve.wait_ge(silu_done[ph], j + 1)
                v.tensor_tensor(hg[:, par, :], ps[:, 2 * par + 1, 0:H], hg[:, par, :], ALU.mult).then_inc(h_done[ph], 1)

            def shared_y(ph, i):
                dve.wait_ge(y_done[ph], i + 1)
                t = i + EARLY * ph
                v.tensor_tensor(hres[:, t, :], ps[:, 5, :], hres[:, t, :], ALU.add).then_inc(y_used[ph], 1)

            def expert_y(b, stored):
                dve.wait_ge(y_done[0], b + (EARLY + 1))
                dve.wait_ge(y_stored, stored)
                v.tensor_copy(yb[:], ps[:, 5, :]).then_inc(y_used[0], 1)

            hidden(0, 0, 0)
            hidden(0, 1, 1)
            dve.wait_ge(sig_done, 1)
            link(v.tensor_tensor(grid(sbias), grid(sc), over_tiles(gb[:]), ALU.add))
            for sel, m, r in ((sel1, m1, r1), (sel2, m2, r2)):
                link(v.tensor_reduce(m, grid(sbias), AX.X, ALU.max))
                link(v.tensor_tensor(grid(t0), grid(sbias), over_experts(m), ALU.is_equal))
                link(v.tensor_tensor(grid(t0), grid(t0), over_tiles(rev), ALU.mult))
                link(v.tensor_reduce(r, grid(t0), AX.X, ALU.max))
                link(v.tensor_tensor(grid(sel), over_tiles(rev), over_experts(r), ALU.is_equal))
                if sel is sel1:
                    link(v.scalar_tensor_tensor(out=sbias, in0=sel1, scalar=NEG, in1=sbias, op0=ALU.mult, op1=ALU.add))
            v.tensor_tensor(msel, sel1, sel2, ALU.add).then_inc(sel_ready, 1)

            for t, sel, c in ((t0, sel1, 0), (t1, sel2, 1)):
                link(v.tensor_tensor(t, sc, sel, ALU.mult))
                link(v.tensor_reduce(wtop[:, c, :], grid(t), AX.X, ALU.add))
            link(v.tensor_tensor(wsum, wtop[:, 0, :], wtop[:, 1, :], ALU.add))
            link(v.reciprocal(wsum, wsum))
            link(v.tensor_tensor(wtop[:], wtop[:], wsum.unsqueeze(1).to_broadcast([P, 2, TT]), ALU.mult))
            hidden(0, 2, 0)
            shared_y(0, 0)
            dve.wait_ge(rank_done, 1)
            tot = ps[:, 7, TT * E:2 * TT * E]
            link(v.tensor_reduce(cnt, tot.rearrange("p (i e) -> p e i", e=E), AX.X, ALU.add))
            ov = over.rearrange("p (e i) -> p e i", i=TT)
            link(v.tensor_tensor(ov, cnt.unsqueeze(2).to_broadcast([P, E, TT]),
                                 thr.unsqueeze(1).to_broadcast([P, E, TT]), ALU.is_gt))
            link(v.tensor_reduce(nblk, ov, AX.X, ALU.add))
            link(v.tensor_tensor_scan(incl, cst[:, C_ONE:C_ONE + E], nblk, 0.0, ALU.mult, ALU.add))
            link(v.tensor_tensor(base0, incl, nblk, ALU.subtract))
            bt = grid(baseT)
            link(v.tensor_scalar(bt[:, 0, :], base0, float(P), None, ALU.mult))
            for i in range(1, TT):
                link(v.tensor_tensor(bt[:, i, :], bt[:, i - 1, :], grid(tot)[:, i - 1, :], ALU.add))
            link(v.tensor_tensor(pos, ps[:, 7, 0:TT * E], baseT, ALU.add))
            for t, sel, c in ((t0, sel1, 0), (t1, sel2, 1)):
                link(v.tensor_tensor(t, pos, sel, ALU.mult))
                link(v.tensor_reduce(slotf[:, c * TT:(c + 1) * TT], grid(t), AX.X, ALU.add))
            v.tensor_copy(slot_i[:].rearrange("p c i -> p (c i)"), slotf).then_inc(slot_ready, 1)
            bc = blkc.rearrange("p (b e) -> p b e", e=E)[0:1]
            link(v.tensor_tensor(bc, incl[0:1].unsqueeze(1).to_broadcast([1, NB + 1, E]),
                                 blki[0:1].unsqueeze(2).to_broadcast([1, NB + 1, E]), ALU.is_le))
            link(v.tensor_reduce(blkf[0:1], bc, AX.X, ALU.add))
            link(v.tensor_scalar(blk[:], blkf[0:1], float(E - 1), None, ALU.min))
            link(v.tensor_scalar(tripc[0:1], blki[0:1, 1:2 * E:2], incl[0:1, E - 1:E], None, ALU.is_lt))
            link(v.tensor_reduce(blkf[0:1, 0:1], tripc[0:1], AX.X, ALU.add))
            v.tensor_scalar(trip[:], blkf[0:1, 0:1], 2.0, None, ALU.mult).then_inc(blk_ready, 1)

            for j in range(3, J0):
                hidden(0, j, j % 2)
                if j % SH == 0:
                    shared_y(0, j // SH - 1)
            hidden(0, J0, 0)
            shared_y(0, EARLY - 1)
            dve.wait_ge(blk_ready, 1)
            last_b = dve.value_load(trip[0:1, 0:1], min_val=TMIN - 1, max_val=NB - 1)
            hidden(0, J0 + 1, 1)
            dve.wait_ge(y_done[0], EARLY + 1)
            v.tensor_copy(yb[:], ps[:, 5, :]).then_inc(y_used[0], 1)
            hidden(0, J0 + 2, 0)
            expert_y(1, 16)
            with dve.Fori(3, last_b + 1, 2) as b:
                for u in range(2):
                    hidden(0, b + (u + J0), (1 + u) % 2)
                    expert_y(b + (u - 1), (b + (u - 1)) * 16)
            hidden(1, 0, 1)
            expert_y(last_b, last_b * 16)

            def combine(i):
                for c in range(2):
                    ins = v.scalar_tensor_tensor(out=hres[:, i, :], in0=yg[:, c, i, :], scalar=wtop[:, c, i:i + 1],
                                                 in1=hres[:, i, :], op0=ALU.mult, op1=ALU.add)
                    if c == 0 or i == TT - 1:
                        link(ins)
                    else:
                        ins.then_inc(out_ready, 1)

            hidden(1, 1, 0)
            hidden(1, 2, 1)
            shared_y(1, 0)
            hidden(1, 3, 0)
            dve.wait_ge(y_used[0], EARLY)
            dve.wait_ge(y_used[1], 1)
            dve.wait_ge(gathered, 2 * TT * 16)
            for i in range(TT):
                combine(i)
            dve.wait_ge(y_done[1], 2)
            v.tensor_tensor(hres[:, TT - 1, :], ps[:, 5, :], hres[:, TT - 1, :], ALU.add).then_inc(out_ready, 1)

        @block.gpsimd
        def _(pool):
            g = nc.gpsimd
            steps = [0]
            g.memset(halfneg[:], -0.5).then_inc(const_ready, 1)
            g.memset(xb[:], 0.0).then_inc(zero_ready, 1)
            g.memset(QT[:, NGRP * TOK:NGRP * TOKP], 0.0)
            g.memset(KT[:, TOK:TOKP], 0.0)
            g.memset(VT[:, TOK:TOKP], 0.0).then_inc(pad_ready, 1)
            pool.wait_ge(const_ready, 1)

            def inv_std(i, nth):
                pool.wait_ge(stats_ready, nth + 1)
                g.tensor_scalar(rstd[:, i:i + 1], mv[:, i, 1:2], EPS, None, ALU.add).then_inc(pool_step, 1)
                steps[0] += 1
                pool.wait_ge(pool_step, steps[0])
                g.tensor_tensor(rstd[:, i:i + 1], rstd[:, i:i + 1], halfneg[:], ALU.pow).then_inc(rstd_ready, 1)

            def rotate(i):
                pool.wait_ge(rope_ready, i + 1)
                if i >= 2:
                    pool.wait_ge(ropeT_ps, i - 1)
                g.tensor_tensor(qkr[i % 2], ropeA, ropeB, ALU.add).then_inc(qkr_ready, 1)

            for i in range(TT):
                inv_std(i, i)
            for i in range(TT):
                rotate(i)

            def spread_v(a):
                n, t = AG[a], TG * a * GQ
                if a >= 2:
                    pool.wait_ge(vB_ps, a - 1)
                src = bass.AP(VT.tensor, VT.offset + t, [list(VT.ap[0]), [GQ, n], [0, NKV], [1, GK]])
                own = bass.AP(headm.tensor, headm.offset, [list(headm.ap[0]), [0, n], [1, NKV], [0, GK]])
                g.tensor_tensor(VD[a % 2][:, 0:n * P].rearrange("p (j n k) -> p j n k", j=n, k=GK), src, own,
                                ALU.mult).then_inc(vd_ready, 1)

            def normalise(a):
                n = AG[a] * NKV
                pool.wait_ge(rden_ready, a + 1)
                p = prob[a % 2][0:QROWS, 0:n * GK].rearrange("p (c k) -> p c k", k=GK)
                g.tensor_tensor(p, p, rden[0:QROWS, a % 2, 0:n].unsqueeze(2).to_broadcast([QROWS, n, GK]), ALU.mult)\
                    .then_inc(prob_ready, 1)

            pool.wait_ge(vT_ready, TT)
            pool.wait_ge(pad_ready, 1)
            pool.wait_ge(l_cst, 16)
            spread_v(0)
            spread_v(1)
            normalise(0)
            normalise(1)
            for a in range(AT):
                if a >= 2:
                    inv_std(a - 2, TT + a - 2)
                if a + 2 < AT:
                    spread_v(a + 2)
                    normalise(a + 2)
            inv_std(TT - 1, 2 * TT - 1)

            pool.wait_ge(zeroed, 32)
            pool.wait_ge(slot_ready, 1)
            for c in range(2):
                for i in range(TT):
                    g.indirect_dma_start(out=x_disp, out_offset=bass.IndirectOffsetOnAxis(
                        ap=slot_i[:, c, i:i + 1].bitcast(U32), axis=0), in_=xn[:, i, :], in_offset=None)\
                        .then_inc(scattered, 16)
            pool.wait_ge(all_stored, 1)
            for i in range(TT):
                for c in range(2):
                    g.indirect_dma_start(out=yg[:, c, i, :], out_offset=None, in_=y_disp,
                                         in_offset=bass.IndirectOffsetOnAxis(
                                             ap=slot_i[:, c, i:i + 1].bitcast(U32), axis=0)).then_inc(gathered, 16)


def constants():
    c = np.zeros((P, C_END), np.float32)
    i = np.arange(P)
    c[:, C_ID:C_ID + P] = i[:, None] == i[None, :]
    c[:, C_TRI:C_TRI + P] = i[:, None] < i[None, :]
    c[:, C_ONE:C_ONE + P] = 1.0
    q, k = np.arange(QROWS) // NGRP, np.arange(GK)
    c[:QROWS, C_MASK:C_MASK + GK] = np.where(q[:, None] // NPOS == k[None, :] // NPOS, 0.0, NEG)
    c[:, C_HEAD:C_HEAD + NKV] = i[:, None] // HD == np.arange(NKV)[None, :]
    c[:, C_REV:C_REV + E] = E - np.arange(E)
    c[:, C_THR:C_THR + TT] = P * np.arange(TT)
    c[:, C_BLK:C_BLK + NB + 1] = np.arange(NB + 1)
    freqs = (1.0 / THETA ** (np.arange(0, HD, 2, dtype=np.float32) / HD)).astype(np.float32)
    emb = np.outer(np.arange(NPOS, dtype=np.float32), freqs).astype(np.float32)
    cos, sin = np.cos(emb), np.sin(emb)
    root = float(HD) ** -0.25
    table = np.stack([np.concatenate([cos, cos], 1), np.concatenate([-sin, sin], 1)], 1) * root
    rows = table[np.arange(TOK) % NPOS].reshape(TT, P, 2 * HD)
    c[:, C_ROPE:C_END] = rows.transpose(1, 0, 2).reshape(P, TT * 2 * HD)
    return c


def kernel(x, L0_tok_W, L0_tok_b, L0_attn_Wq, L0_attn_Wk, L0_attn_Wv, L0_attn_Wo, L0_ffn_gate_w,
           L0_ffn_gate_bias, L0_ffn_shared_gw, L0_ffn_shared_dw, L0_ffn_up_w, L0_ffn_down_w):
    import concourse.bacc as bacc
    from concourse.bass_utils import run_bass_kernel_spmd

    a = {n: np.asarray(v) for n, v in dict(
        x=x, tw=L0_tok_W, tb=L0_tok_b, wq=L0_attn_Wq, wk=L0_attn_Wk, wv=L0_attn_Wv, wo=L0_attn_Wo,
        gw=L0_ffn_gate_w, gb=L0_ffn_gate_bias, sg=L0_ffn_shared_gw, sd=L0_ffn_shared_dw, up=L0_ffn_up_w,
        dn=L0_ffn_down_w).items()}

    def chunks(m):
        return m.reshape(-1, P, m.shape[1]).transpose(1, 0, 2)

    wq = a["wq"].reshape(D, NKV, NGRP, HD).transpose(0, 2, 1, 3).reshape(D, D)
    wqkv = chunks(np.concatenate([wq, a["wk"], a["wv"]], 1))
    wo = a["wo"].reshape(NKV, NGRP, HD, D).transpose(0, 2, 1, 3).reshape(P, NGRP, D)
    ups = [np.concatenate([a["sg"][(SH + s) * H:(SH + s + 1) * H], a["sg"][s * H:(s + 1) * H]]) for s in range(SH)]
    dns = [a["sd"][:, s * H:(s + 1) * H] for s in range(SH)]
    ups += [a["up"][e] for e in range(E)]
    dns += [a["dn"][e] for e in range(E)]
    wa = np.stack([np.concatenate([chunks(u.T).reshape(P, UPW), chunks(d.T[:2 * P]).reshape(P, 2 * D)], 1)
                   for u, d in zip(ups, dns)])
    wb = np.stack([d.T[2 * P:] for d in dns])
    ins = [("xT", a["x"][:, :, 0].T), ("tok_w", a["tw"].T), ("tok_b", a["tb"]), ("consts", constants()),
           ("wqkv", wqkv), ("wo", wo), ("gate_w", chunks(a["gw"].T)), ("gate_b", a["gb"]), ("wa", wa), ("wb", wb)]

    nc = bacc.Bacc("TRN2", target_bir_lowering=False, num_devices=1)
    arrays, args = {}, []
    for name, v in ins:
        v = np.ascontiguousarray(v)
        arrays[name + "_in"] = v
        args.append(nc.dram_tensor(name + "_in", v.shape, mybir.dt.from_np(v.dtype), kind="ExternalInput").ap())
    out = nc.dram_tensor("out_0", (BATCH, NPOS, D), F32, kind="ExternalOutput").ap()
    build(nc, *args, out)
    r = run_bass_kernel_spmd(nc, [arrays], core_ids=[0])
    return r.results[0]["out_0"]
```

```python
from contextlib import ExitStack

import numpy as np

import concourse.bass as bass
from concourse import mybir
from concourse.alu_op_type import AluOpType as ALU

F32 = mybir.dt.float32
F32R = mybir.dt.float32r
BF16 = mybir.dt.bfloat16
I32 = mybir.dt.int32
U32 = mybir.dt.uint32
ACT = mybir.ActivationFunctionType
AX = mybir.AxisListType

P = 128
BATCH, SEQ = 64, 750
PATCH, STRIDE = 128, 64
NPOS = (SEQ - PATCH) // STRIDE + 1
TOK = BATCH * NPOS
D = 512
KC = D // P
TT = TOK // P
NKV, NGRP, HD = 4, 4, 32
THETA = 10000.0
QK = (NKV * NGRP + NKV) * HD
QKV = QK + NKV * HD
EPS = 1e-5

GB = 3
GQ = GB * NPOS
GK = 32
NG = -(-BATCH // GB)
TG = 4
AT = -(-NG // TG)
AG = [min(TG, NG - TG * a) for a in range(AT)]
TOKP = NG * GQ + GK
QROWS = NGRP * GQ
NEG = -1e30

E = 8
H = 352
SH = 2
HC = [P, P, H - 2 * P]
UPW = KC * 2 * H
WA = UPW + 2 * D
SLOT = UPW + 3 * D
NSLOT = SH + E
NB = (2 * TOK + E * (P - 1)) // P
EARLY = 3
J0 = SH * EARLY
LATE = SH * (TT - EARLY)
TMIN = 2 * TOK // P
PROJ_SLOT, SCORE_SLOT = 4, 5
EARLY_SLOT = 8
PLACES = [4, 5, 6, 7, 8, 9, 2, 3]
WRAP = 6
HI_BITS = -4096
WCH = [2 * H] * KC + [D] * 3

W_SPLITS = [2, 2, 2, 1] + [0, 1, 1, 1, 1, 1] + [2]
assert sum(W_SPLITS) == SH * len(WCH)

C_ID, C_TRI, C_ONE, C_MASK = 0, P, 2 * P, 3 * P
C_REV = C_MASK + GK
C_THR = C_REV + E
C_BLK = C_THR + TT
C_HEAD = C_BLK + NB + 1
C_ROPE = C_HEAD + NKV
C_END = C_ROPE + TT * 2 * HD


def build(nc, xT, tok_w, tok_b, consts, wqkv, wo, gate_w, gate_b, wa, wb, out):
    x_disp = nc.dram_tensor("x_disp", [(NB + 1) * P, D], F32, kind="Internal").ap()
    y_disp = nc.dram_tensor("y_disp", [NB * P, D], F32, kind="Internal").ap()
    out_rows = out.rearrange("b n d -> (b n) d")

    ctx = ExitStack()
    with ctx:
        def sb(name, shape, dt=F32):
            return ctx.enter_context(nc.sbuf_tensor(name, shape, dt))

        def sem(name):
            return ctx.enter_context(nc.semaphore(name))

        AUX = 2 * WCH[0] + 3 * P
        with ExitStack() as first:
            split = [first.enter_context(nc.sbuf_tensor(f"split{s}", [P, SLOT], F32R)) for s in range(NSLOT)]
            split.append(first.enter_context(nc.sbuf_tensor("split_aux", [P, AUX], F32R)))
        shared_w = sb("shared_w", [P, SH * SLOT])
        expert_w = sb("expert_w", [P, E * SLOT])
        aux = sb("aux", [P, AUX])

        def f32(o, n, rows=P):
            for t, start in ((aux, NSLOT * SLOT), (expert_w, SH * SLOT), (shared_w, 0)):
                if o >= start:
                    return t[0:rows, o - start:o - start + n]

        def parts(o, n, rows=P):
            s = min(o // SLOT, NSLOT)
            return split[s][0:rows, o - s * SLOT:o - s * SLOT + n]

        wtmp_at = NSLOT * SLOT
        wtmp = [f32(wtmp_at + u * WCH[0], WCH[0]) for u in range(2)]
        hT_at = wtmp_at + 2 * WCH[0]
        hT = f32(hT_at, 3 * P).rearrange("p (c t) -> p c t", c=3)
        hres = sb("hres", [P, TT, D])
        xn2T = sb("xn2T", [P, KC, TOK])
        xb = sb("xb", [P, D])
        xbT = sb("xbT", [P, KC, P])
        hg = sb("hg", [P, 3 * P])
        yb = sb("yb", [P, D])
        cst = sb("cst", [P, C_ROPE])
        identb = sb("identb", [P, P], BF16)
        maskb = sb("maskb", [P, GK], BF16)
        gw = sb("gw", [P, KC, E])
        gb = sb("gb", [P, E])
        halfneg = sb("halfneg", [P, 1])
        stats = sb("stats", [P, 2, 6])
        mv = sb("mv", [P, TT, 2])
        rstd = sb("rstd", [P, TT])
        nmax = sb("nmax", [P, 2, TG * NKV])
        esum = sb("esum", [P, 2, TG * NKV])
        rden = sb("rden", [P, 2, TG * NKV])
        slot_i = sb("slot_i", [P, 2, TT], I32)
        wtop = sb("wtop", [P, 2, TT])
        blk = sb("blk", [1, NB + 1], I32)
        place = sb("place", [1, NB + 1], I32)
        trip = sb("trip", [1, 2], I32)
        ps = ctx.enter_context(nc.psum_tensor("ps", [P, 8, 512], F32))

        ident = cst[:, C_ID:C_ID + P]
        tri = cst[:, C_TRI:C_TRI + P]
        ones = cst[:, C_ONE:C_ONE + P]
        rev = cst[:, C_REV:C_REV + E]
        thr = cst[:, C_THR:C_THR + TT]
        blki = cst[:, C_BLK:C_BLK + NB + 1]
        headm = cst[:, C_HEAD:C_HEAD + NKV]

        at = [0]

        def front(n):
            at[0] += n
            return f32(at[0] - n, n)

        def start(s):
            assert at[0] <= s * SLOT
            at[0] = s * SLOT

        start(PROJ_SLOT)
        wqkv_sb = front(KC * QKV).rearrange("p (k n) -> p k n", k=KC)
        praw = front(NPOS * BATCH)
        pT = front(TOK)
        ropeA, ropeB = praw, pT
        start(SCORE_SLOT)
        QT = front(NGRP * TOKP)
        KD = [front(TG * P) for _ in range(2)]
        start(SCORE_SLOT + 1)
        VD, VB = ([front(TG * P) for _ in range(2)] for _ in range(2))
        wo_sb = front(NGRP * D).rearrange("p (g n) -> p g n", g=NGRP)
        start(SCORE_SLOT + 2)
        xnT = front(KC * TOKP).rearrange("p (k t) -> p k t", k=KC)
        yT = xnT
        PT = [front(TG * QROWS) for _ in range(2)]
        start(EARLY_SLOT)
        tokw = front(D)
        tokb = front(D)
        rope = front(TT * 2 * HD).rearrange("p (i c d) -> p i c d", i=TT, c=2)
        qkv = [front(QKV) for _ in range(2)]
        at[0] = EARLY_SLOT * SLOT + EARLY * 2 * D
        KT = front(TOKP)
        start(NSLOT - 1)
        VT = front(TOKP)
        xn = front(TT * D).rearrange("p (i d) -> p i d", i=TT)
        prob_at = at[0]
        prob = [front(TG * P) for _ in range(2)]
        assert at[0] <= NSLOT * SLOT
        at[0] = prob_at

        def routing(n):
            return front(n)

        sc, sbias, t0, t1, sel1, sel2, msel, pos = (routing(TT * E) for _ in range(8))
        m1, m2, r1, r2, wsum = (routing(TT) for _ in range(5))
        cnt, nblk, incl, base0 = (routing(E) for _ in range(4))
        over = routing(E * TT)
        baseT = routing(TT * E)
        blkc = routing((NB + 1) * E)
        blkf = routing(NB + 1)
        slotf = routing(2 * TT)
        assert at[0] <= NSLOT * SLOT
        yg = f32(6 * SLOT, 2 * TT * D).rearrange("p (c i d) -> p c i d", c=2, i=TT)

        def x_at(i):
            if i < EARLY:
                return EARLY_SLOT * SLOT + i * 2 * D
            return wtmp_at if i == EARLY else EARLY_SLOT * SLOT

        def xh(i):
            return parts(x_at(i), D).rearrange("p (k t) -> p k t", k=KC)

        def xl(i):
            return parts(x_at(i) + D, D).rearrange("p (k t) -> p k t", k=KC)

        hh = parts(hT_at, 3 * P)
        hl_at = wtmp_at + 2 * D
        hl = parts(hl_at, 3 * P)
        assert hl_at + 3 * P <= hT_at

        def tmp(late, n):
            return (xb if late else yb)[:, 0:n]

        lo_early, lo_late = (2, 3), (4, 5)

        def wchunk(s, n, view):
            return view(s * SLOT + sum(WCH[:n]), WCH[n], HC[2] if n == len(WCH) - 1 else P)

        l_x, l_tokw, l_tokb, l_cst, l_rope = (sem(n) for n in ("l_x", "l_tokw", "l_tokb", "l_cst", "l_rope"))
        l_qkv, l_wo, l_gate = sem("l_qkv"), sem("l_wo"), sem("l_gate")
        l_slot = [sem(f"l_slot{s}") for s in range(NSLOT)]
        l_last = [[sem(f"l_last{e}_{u}") for u in range(2)] for e in range(E)]
        l_again = sem("l_again0"), sem("l_again1")
        zeroed, scattered, xb_loaded = sem("zeroed"), sem("scattered"), sem("xb_loaded")
        experts_loaded = sem("experts_loaded")
        all_stored = sem("all_stored")
        y_stored, out_stored = sem("y_stored"), sem("out_stored")
        gathered = [sem(f"gathered{i}") for i in range(TT)]
        (tok_done, xnT_ps, qk_done, ropeT_ps, s_done, vB_ps, pT_ps, pv_done, wo_done, x2T_ps,
         logit_done, rank_done, xbT_ps) = (sem(n) for n in (
             "tok_done", "xnT_ps", "qk_done", "ropeT_ps", "s_done", "vB_ps", "pT_ps", "pv_done", "wo_done",
             "x2T_ps", "logit_done", "rank_done", "xbT_ps"))
        (bf_ready, xnT_ready, qkT_ready, v_ready, exp_done, yT_ready, x2T_ready, sig_done, xbT_ready) = (
            sem(n) for n in ("bf_ready", "xnT_ready", "qkT_ready", "v_ready", "exp_done", "yT_ready", "x2T_ready",
                             "sig_done", "xbT_ready"))
        (patch_ready, tok_used, stats_ready, xn_ready, rope_ready, kd_ready, vb_ready, sub_done, rden_ready, pT_ready,
         resid_done, xn2_ready, sel_ready, slot_ready, blk_ready, out_ready, dve_step) = (sem(n) for n in (
             "patch_ready", "tok_used", "stats_ready", "xn_ready", "rope_ready", "kd_ready", "vb_ready", "sub_done",
             "rden_ready", "pT_ready", "resid_done", "xn2_ready", "sel_ready", "slot_ready", "blk_ready", "out_ready", "dve_step"))
        const_ready, zero_ready, pad_ready, rstd_ready, qkr_ready, vd_ready, prob_ready, pool_step = (sem(n) for n in (
            "const_ready", "zero_ready", "pad_ready", "rstd_ready", "qkr_ready", "vd_ready", "prob_ready", "pool_step"))

        def pair(name):
            return [sem(name), sem("late_" + name)]

        g_done, u_done, hT_ps, y_done = pair("g_done"), pair("u_done"), pair("hT_ps"), pair("y_done")
        silu_done, hT_ready = pair("silu_done"), pair("hT_ready")
        h_done, y_used = pair("h_done"), pair("y_used")
        htmp_ready, hl_ready = pair("htmp_ready"), pair("hl_ready")
        wtmp_ready, xtmp_ready, xl_ready = (sem(n) for n in ("wtmp_ready", "xtmp_ready", "xl_ready"))
        wl_ready = [sem(f"wl_ready{s}") for s in range(SH)]
        wh_ready, xh_ready = sem("wh_ready"), sem("xh_ready")
        two_through = sem("two_through")
        late_wl_ready = sem("late_wl_ready")

        def late_bank(ph, j):
            return 2 * (j % 2) if ph else 0

        def tok_bank(i):
            return (0, 1, 6, 7)[i % 4]

        def proj_bank(i):
            return (4, 6, 0)[i % 3]

        def tiles_of(a):
            return min(TT, -(-(TG * (a + 1) * GQ + GK) // P))

        def up(s, k, half):
            return parts(s * SLOT + (2 * k + half) * H, H)

        def down(s, c):
            return parts(s * SLOT + UPW + c * D, D, HC[c])

        block = ctx.enter_context(nc.Block())

        @block.sync
        def _(sp):
            sp.dma_start(praw.rearrange("p (n b) -> p n b", n=NPOS),
                         bass.AP(xT.tensor, 0, [[BATCH, P], [STRIDE * BATCH, NPOS], [1, BATCH]])).then_inc(l_x, 16)
            sp.dma_start(tokb, bass.AP(tok_b.tensor, 0, [[0, P], [1, D]])).then_inc(l_tokb, 16)
            sp.dma_start(wqkv_sb, wqkv).then_inc(l_qkv, 16)
            sp.dma_start(gw[:], gate_w).then_inc(l_gate, 16)
            sp.dma_start(gb[:], bass.AP(gate_b.tensor, 0, [[0, P], [1, E]])).then_inc(l_gate, 16)

            def load_slot(s, w):
                sp.dma_start(f32(s * SLOT, WA), wa[w]).then_inc(l_slot[s], 16)
                sp.dma_start(f32(s * SLOT + WA, D, HC[2]), wb[w]).then_inc(l_slot[s], 16)

            def load_experts(first, last):
                for e in range(first, last):
                    load_slot(PLACES[e], SH + e)

            load_slot(0, 0)
            sp.dma_start(wo_sb, wo).then_inc(l_wo, 16)
            load_slot(1, 1)
            sp.wait_ge(zero_ready, 1)
            sp.dma_start(x_disp.rearrange("(b p) d -> p b d", p=P),
                         bass.AP(xb, 0, [[D, P], [0, NB + 1], [1, D]])).then_inc(zeroed, 16)
            sp.dma_start(y_disp[TMIN * P:, :].rearrange("(b p) d -> p b d", p=P),
                         bass.AP(xb, 0, [[D, P], [0, NB - TMIN], [1, D]])).then_inc(zeroed, 16)
            sp.wait_ge(ropeT_ps, TT)
            load_experts(0, 1)
            sp.wait_ge(s_done, AT)
            load_experts(1, 2)
            sp.wait_ge(wo_done, TT)
            load_experts(2, PLACES.index(EARLY_SLOT))
            sp.wait_ge(scattered, 2 * TT * 16)
            sp.wait_ge(blk_ready, 1)
            sp.dma_start(xb[:], x_disp[0:P, :]).then_inc(xb_loaded, 16)
            last_b = sp.value_load(trip[0:1, 0:1], min_val=TMIN - 1, max_val=NB - 1)

            def load_x(b):
                sp.wait_ge(xbT_ps, b)
                sp.dma_start(xb[:], x_disp[bass.ds(b * P, P), :]).then_inc(xb_loaded, 16)

            def store_y(b):
                sp.wait_ge(y_used[0], b + (EARLY + 1))
                sp.dma_start(y_disp[bass.ds(b * P, P), :], yb[:]).then_inc(y_stored, 16)

            load_x(1)
            load_experts(5, 6)
            load_x(2)
            with sp.Fori(3, last_b + 2) as b:
                load_x(b)
                store_y(b - 3)
            store_y(last_b - 1)
            store_y(last_b)
            sp.wait_ge(y_stored, last_b * 16 + 16)
            sp.sem_inc(all_stored, 1)
            for i in range(TT):
                sp.wait_ge(out_ready, i + 1)
                sp.dma_start(out_rows[i * P:(i + 1) * P, :], hres[:, i, :]).then_inc(out_stored, 16)
            sp.wait_ge(out_stored, TT * 16)

        @block.tensor
        def _(pe):
            mm = nc.tensor.matmul

            def transposes(dst, srcs, ident_ap):
                for o, src in zip(dst, srcs):
                    last = nc.tensor.transpose(o, src, ident_ap)
                return last

            pe.wait_ge(patch_ready, 1)
            pe.wait_ge(l_tokw, 16)
            def embed(i):
                if i >= 4:
                    pe.wait_ge(tok_used, i - 3)
                mm(ps[:, tok_bank(i), :], pT[:, i * P:(i + 1) * P], tokw, start=True, stop=True).then_inc(tok_done, 1)

            for i in range(TT - 1):
                embed(i)

            def norm_T(i):
                pe.wait_ge(xn_ready, i + 1)
                pe.wait_ge(l_cst, 16)
                if i >= 2:
                    pe.wait_ge(xnT_ready, i - 1)
                b = 2 + i % 2
                transposes([ps[:, b, k * P:(k + 1) * P] for k in range(KC)],
                           [xn[:, i, k * P:(k + 1) * P] for k in range(KC)], ident).then_inc(xnT_ps, 1)

            def project(i):
                pe.wait_ge(xnT_ready, i + 1)
                pe.wait_ge(l_qkv, 16)
                if i >= 1:
                    pe.wait_ge(tok_used, TT)
                if i >= 3:
                    pe.wait_ge(qkT_ready, i - 2)
                b = proj_bank(i)
                for c in range(2):
                    if i == 0 and c == 1:
                        norm_T(1)
                    for k in range(KC):
                        last = mm(ps[:, b + c, 0:QKV // 2], xnT[:, k, i * P:(i + 1) * P],
                                  wqkv_sb[:, k, c * (QKV // 2):(c + 1) * (QKV // 2)], start=(k == 0), stop=(k == KC - 1))
                last.then_inc(qk_done, 1)

            def rope_T(i):
                pe.wait_ge(qkr_ready, i + 1)
                pe.wait_ge(v_ready, i + 1)
                b = proj_bank(i)
                r = qkv[i % 2]
                transposes([ps[:, b + c // 4, (c % 4) * P:(c % 4 + 1) * P] for c in range(6)],
                           [r[:, c * P:(c + 1) * P] for c in range(6)], ident).then_inc(ropeT_ps, 1)

            def scores(a):
                n = AG[a] * P
                if a >= 2:
                    pe.wait_ge(sub_done, a - 1)
                mm(ps[0:QROWS, a % 2, 0:n], identb[0:QROWS, 0:QROWS],
                   maskb[0:QROWS, :].unsqueeze(1).to_broadcast([QROWS, AG[a] * NKV, GK]), start=True, stop=False)
                pe.wait_ge(kd_ready, a + 1)
                for j in range(AG[a]):
                    t = (TG * a + j) * GQ
                    last = mm(ps[0:QROWS, a % 2, j * P:(j + 1) * P], QT[:, t * NGRP:(t + GQ) * NGRP], KD[a % 2][:, j * P:(j + 1) * P],
                              start=False, stop=(j == AG[a] - 1))
                last.then_inc(s_done, 1)

            def value_blocks(a):
                pe.wait_ge(vd_ready, a + 1)
                if a >= 1:
                    pe.wait_ge(vb_ready, a)
                transposes([ps[:, 2, j * P:(j + 1) * P] for j in range(AG[a])],
                           [VD[a % 2][:, j * P:(j + 1) * P] for j in range(AG[a])], ident).then_inc(vB_ps, 1)

            def prob_T(a):
                pe.wait_ge(prob_ready, a + 1)
                if a >= 2:
                    pe.wait_ge(pT_ready, a - 1)
                transposes([ps[:, 4 + a % 2, j * QROWS:(j + 1) * QROWS] for j in range(AG[a])],
                           [prob[a % 2][0:QROWS, j * P:(j + 1) * P] for j in range(AG[a])],
                           ident[0:QROWS, 0:QROWS]).then_inc(pT_ps, 1)

            def prob_v(a):
                pe.wait_ge(pT_ready, a + 1)
                pe.wait_ge(vb_ready, a + 1)
                if a >= 1:
                    pe.wait_ge(yT_ready, a)
                for j in range(AG[a]):
                    c = slice(j * QROWS, (j + 1) * QROWS)
                    last = mm(ps[:, 6, c], VB[a % 2][:, j * P:(j + 1) * P], PT[a % 2][:, c], start=True, stop=True)
                last.then_inc(pv_done, 1)

            def out_proj(i):
                pe.wait_ge(yT_ready, min(i + 2, AT))
                pe.wait_ge(l_wo, 16)
                pe.wait_ge(resid_done, i) if i >= 1 else pe.wait_ge(xnT_ready, TT)
                for g in range(NGRP):
                    last = mm(ps[:, 3, :], yT[:, g, i * P:(i + 1) * P], wo_sb[:, g, :],
                              start=(g == 0), stop=(g == NGRP - 1))
                last.then_inc(wo_done, 1)

            def norm2_T(i):
                pe.wait_ge(xn2_ready, i + 1)
                if i >= 1:
                    pe.wait_ge(x2T_ready, i)
                transposes([ps[:, 7, k * P:(k + 1) * P] for k in range(KC)],
                           [xn[:, i, k * P:(k + 1) * P] for k in range(KC)], ident).then_inc(x2T_ps, 1)

            norm_T(0)
            embed(TT - 1)
            for i in range(TT + 1):
                if 1 < i + 1 < TT:
                    norm_T(i + 1)
                if i >= 2:
                    rope_T(i - 2)
                if i < TT:
                    project(i)
            pe.wait_ge(bf_ready, 1)
            pe.wait_ge(xnT_ready, TT)
            pe.wait_ge(qkT_ready, tiles_of(1))
            scores(0)
            value_blocks(0)
            scores(1)
            value_blocks(1)
            rope_T(TT - 1)
            pe.wait_ge(qkT_ready, TT)
            for a in range(AT):
                if a + 2 < AT:
                    scores(a + 2)
                prob_T(a)
                if a >= 2:
                    out_proj(a - 2)
                prob_v(a)
                if a + 2 < AT:
                    value_blocks(a + 2)
                if a >= 3:
                    norm2_T(a - 3)
            out_proj(TT - 1)
            norm2_T(TT - 2)

            def logits(i, k):
                if k == 0:
                    pe.wait_ge(x2T_ready, i + 1)
                last = mm(ps[:, 6, i * E:(i + 1) * E], xn2T[:, k, i * P:(i + 1) * P], gw[:, k, :],
                          start=(k == 0), stop=(k == KC - 1))
                if k == KC - 1:
                    last.then_inc(logit_done, 1)

            def ranks():
                pe.wait_ge(sel_ready, 1)
                mm(ps[:, 7, 0:TT * E], tri, msel, start=True, stop=True)
                mm(ps[:, 7, TT * E:2 * TT * E], ones, msel, start=True, stop=True).then_inc(rank_done, 1)

            def gate_up(ph, half, xk, w):
                for k in range(KC):
                    last = mm(ps[:, half, 0:H], xk(k), w(k, half), start=(k == 0), stop=(k == KC - 1))
                last.then_inc((u_done if half else g_done)[ph], 1)

            def hidden_T(ph, j):
                for c in range(3):
                    last = nc.tensor.transpose(ps[:, 4, c * P:(c + 1) * P], hg[:, c * P:(c + 1) * P], ident)
                last.then_inc(hT_ps[ph], 1)

            def down_proj(ph, j, w):
                pe.wait_ge(hT_ready[ph], j + 1)
                for c in range(3):
                    last = mm(ps[:, 5, :], hT[0:HC[c], c, :], w(c), start=(c == 0), stop=(c == 2))
                last.then_inc(y_done[ph], 1)

            def block_T(b):
                pe.wait_ge(xb_loaded, (b + 1) * 16)
                transposes([ps[:, 7, k * P:(k + 1) * P] for k in range(KC)],
                           [xb[:, k * P:(k + 1) * P] for k in range(KC)], ident).then_inc(xbT_ps, 1)

            def split_product(o, x_hi, x_lo, w_hi, w_lo, first, final):
                mm(o, x_hi, w_hi, start=first, stop=False)
                mm(o, x_hi, w_lo, start=False, stop=False)
                return mm(o, x_lo, w_hi, start=False, stop=final)

            def shared_gate_up(ph, j, half, routed=()):
                chunks = [(t, k) for t in routed for k in range(KC)]
                per = len(routed)
                i, s = j // SH + EARLY * ph, j % SH
                lo = (lo_early, lo_late)[ph][s]
                if half == 0 and s == 0:
                    pe.wait_ge(xh_ready, i + 1)
                    pe.wait_ge(xl_ready, i + 1)
                for k in range(KC):
                    last = split_product(ps[:, late_bank(ph, j) + half, 0:H], xh(i)[:, k, :], xl(i)[:, k, :], up(s, k, half),
                                         up(lo, k, half), k == 0, k == KC - 1)
                    for c in chunks[k * per:(k + 1) * per]:
                        logits(*c)
                last.then_inc((u_done if half else g_done)[ph], 1)

            def shared_down(ph, j):
                s = j % SH
                lo = (lo_early, lo_late)[ph][s]
                if s == 0 and j > 0:
                    pe.wait_ge(y_used[ph], j // SH)
                pe.wait_ge(hl_ready[ph], j + 1)
                pe.wait_ge(hT_ready[ph], j + 1)
                for c in range(3):
                    t = slice(c * P, (c + 1) * P)
                    last = split_product(ps[:, 5, :], hh[0:HC[c], t], hl[0:HC[c], t], down(s, c),
                                         down(lo, c), s == 0 and c == 0, s == SH - 1 and c == 2)
                if s == SH - 1:
                    last.then_inc(y_done[ph], 1)


            pe.wait_ge(sub_done, AT)
            for j in range(J0):
                if j < SH:
                    pe.wait_ge(wh_ready, (j + 1) * len(WCH))
                if j > 0:
                    pe.wait_ge(h_done[0], j)
                if j == 0:
                    pe.wait_ge(l_gate, 32)
                    pe.wait_ge(yT_ready, AT)
                shared_gate_up(0, j, 0, ((0, 1), (TT - 1,))[j] if j < 2 else ())
                if j > 0:
                    hidden_T(0, j - 1)
                shared_gate_up(0, j, 1, (2, 3) if j == 0 else ())
                if j == 0:
                    norm2_T(TT - 1)
                    pe.wait_ge(pT_ready, AT)
                if j == 2:
                    ranks()
                if j > 0:
                    shared_down(0, j - 1)

            def entry(table, b, n):
                return pe.value_load(table[0:1, b:b + 1] if isinstance(b, int) else table[0:1, bass.ds(b, 1)],
                                     min_val=0, max_val=n)

            def expert_up(s):
                return lambda k, half: expert_w[:, bass.ds(s * SLOT + (k * 2 * H + half * H), H)]

            def expert_down(s):
                return lambda c: expert_w[0:HC[c], bass.ds(s * SLOT + (UPW + c * D), D)]

            def expert_step(b, before=None):
                e, w = entry(blk, b, E - 1), expert_up(entry(place, b, E - 1))
                pe.wait_ge(experts_loaded, e + 1)
                pe.wait_ge(xbT_ready, b + 1)
                pe.wait_ge(h_done[0], b + J0)
                gate_up(0, 0, lambda k: xbT[:, k, :], w)
                if before is not None:
                    hidden_T(0, b + (J0 - 1))
                gate_up(0, 1, lambda k: xbT[:, k, :], w)
                block_T(b + 1)
                if before is not None:
                    expert_tail(before)

            def expert_tail(b):
                w = expert_down(entry(place, b, E - 1))
                pe.wait_ge(y_used[0], b + EARLY)
                down_proj(0, b + J0, w)

            pe.wait_ge(slot_ready, 1)
            pe.wait_ge(h_done[0], J0)
            hidden_T(0, J0 - 1)
            block_T(0)
            shared_down(0, J0 - 1)
            pe.wait_ge(blk_ready, 1)
            expert_step(0)
            last_b = pe.value_load(trip[0:1, 0:1], min_val=TMIN - 1, max_val=NB - 1)
            with pe.Fori(1, last_b + 1) as b:
                expert_step(b, b - 1)

            i, bank = EARLY, ps[:, 0, 0:H]
            pe.wait_ge(resid_done, TT)
            pe.wait_ge(vb_ready, AT)
            pe.wait_ge(h_done[0], last_b + (J0 + 1))
            hidden_T(0, last_b + J0)
            pe.wait_ge(xh_ready, i + 1)
            pe.wait_ge(xl_ready, i + 1)
            for k in range(KC):
                mm(bank, xh(i)[:, k, :], up(0, k, 0), start=(k == 0), stop=False)
                mm(bank, xl(i)[:, k, :], up(0, k, 0), start=False, stop=False)
            expert_tail(last_b)
            pe.wait_ge(late_wl_ready, SH * len(WCH))
            for k in range(KC):
                last = mm(bank, xh(i)[:, k, :], up(lo_late[0], k, 0), start=False, stop=(k == KC - 1))
            last.then_inc(g_done[1], 1)
            shared_gate_up(1, 0, 1)
            for j in range(1, LATE):
                shared_gate_up(1, j, 0)
                pe.wait_ge(h_done[1], j)
                hidden_T(1, j - 1)
                shared_gate_up(1, j, 1)
                if j == 1:
                    pe.wait_ge(y_used[0], last_b + (EARLY + 1))
                shared_down(1, j - 1)
            pe.wait_ge(h_done[1], LATE)
            hidden_T(1, LATE - 1)
            shared_down(1, LATE - 1)

        @block.scalar
        def _(act):
            act.dma_start(tokw, tok_w).then_inc(l_tokw, 16)
            act.dma_start(cst[:], consts[:, 0:C_ROPE]).then_inc(l_cst, 16)
            act.dma_start(rope, consts[:, C_ROPE:C_END].rearrange("p (i c d) -> p i c d", i=TT, c=2)).then_inc(l_rope, 16)
            copy = nc.scalar.copy
            act.wait_ge(l_cst, 16)
            copy(identb[:], ident)
            copy(maskb[:], cst[:, C_MASK:C_MASK + GK]).then_inc(bf_ready, 1)

            def norm_T(i):
                act.wait_ge(xnT_ps, i + 1)
                copy(xnT[:, :, i * P:(i + 1) * P], ps[:, 2 + i % 2, :].rearrange("p (k t) -> p k t", k=KC))\
                    .then_inc(xnT_ready, 1)

            def rope_T(i):
                act.wait_ge(ropeT_ps, i + 1)
                b = proj_bank(i)
                copy(QT[:, i * P * NGRP:(i + 1) * P * NGRP].rearrange("p (t g) -> p g t", g=NGRP),
                     ps[:, b, :].rearrange("p (g t) -> p g t", g=NGRP))
                copy(KT[:, i * P:(i + 1) * P], ps[:, b + 1, 0:P])
                copy(VT[:, i * P:(i + 1) * P], ps[:, b + 1, P:2 * P]).then_inc(qkT_ready, 1)

            def values(i):
                act.wait_ge(rope_ready, i + 1)
                if i >= 2:
                    act.wait_ge(ropeT_ps, i - 1)
                copy(qkv[i % 2][:, QK:], ps[:, proj_bank(i) + 1, QK - QKV // 2:QKV // 2]).then_inc(v_ready, 1)

            def weights_hi(n):
                act.wait_ge(wl_ready[n // len(WCH)], n % len(WCH) + 1)
                o, t = wchunk(n // len(WCH), n % len(WCH), parts), wtmp[n % 2]
                copy(o, t[0:o.shape[0], 0:o.shape[1]]).then_inc(wh_ready, 1)

            norm_T(0)
            norm_T(1)
            norm_T(2)
            values(0)
            norm_T(3)
            chunk = 0
            for i in range(TT - 1):
                rope_T(i)
                for n in range(W_SPLITS[i]):
                    weights_hi(chunk + n)
                chunk += W_SPLITS[i]
                values(i + 1)
                if i + 4 < TT:
                    norm_T(i + 4)

            def exps(a):
                n = AG[a] * P
                act.wait_ge(sub_done, a + 1)
                p = prob[a % 2][0:QROWS, 0:n]
                nc.scalar.activation(p, p, ACT.Exp).then_inc(exp_done, 1)

            def prob_T(a):
                act.wait_ge(pT_ps, a + 1)
                if a >= 2:
                    act.wait_ge(pv_done, a - 1)
                copy(PT[a % 2][:, 0:AG[a] * QROWS], ps[:, 4 + a % 2, 0:AG[a] * QROWS]).then_inc(pT_ready, 1)

            def values_out(a):
                act.wait_ge(pv_done, a + 1)
                t = TG * a * GQ
                o = yT[:, :, t:t + AG[a] * GQ]
                copy(o, ps[:, 6, 0:AG[a] * QROWS].rearrange("p (t g) -> p g t", g=NGRP)).then_inc(yT_ready, 1)

            def norm2_T(i):
                act.wait_ge(x2T_ps, i + 1)
                copy(xn2T[:, :, i * P:(i + 1) * P], ps[:, 7, :].rearrange("p (k t) -> p k t", k=KC))\
                    .then_inc(x2T_ready, 1)

            def value_blocks(a):
                act.wait_ge(vB_ps, a + 1)
                if a >= 2:
                    act.wait_ge(pv_done, a - 1)
                copy(VB[a % 2][:, 0:AG[a] * P], ps[:, 2, 0:AG[a] * P]).then_inc(vb_ready, 1)

            def rows_hi(i):
                act.wait_ge(xtmp_ready, i + 1)
                copy(xh(i).rearrange("p k t -> p (k t)"), tmp(i == TT - 1, D)).then_inc(xh_ready, 1)

            value_blocks(0)
            value_blocks(1)
            exps(0)
            rope_T(TT - 1)
            exps(1)
            for a in range(AT):
                prob_T(a)
                if a + 2 < AT:
                    exps(a + 2)
                values_out(a)
                if a + 2 < AT:
                    value_blocks(a + 2)
                if a >= 3:
                    norm2_T(a - 3)
                for n in range(W_SPLITS[TT - 1 + a]):
                    weights_hi(chunk + n)
                chunk += W_SPLITS[TT - 1 + a]
                if a >= 4:
                    rows_hi(a - 4)
            norm2_T(TT - 2)
            rows_hi(AT - 4)
            for n in range(W_SPLITS[-1]):
                weights_hi(chunk + n)

            def silu(ph, j):
                act.wait_ge(g_done[ph], j + 1)
                nc.scalar.activation(hg[:, 0:H], ps[:, late_bank(ph, j), 0:H], ACT.Silu).then_inc(silu_done[ph], 1)

            def hidden_T(j):
                act.wait_ge(hT_ps[0], j + 1)
                copy(hT.rearrange("p c t -> p (c t)"), ps[:, 4, 0:3 * P]).then_inc(hT_ready[0], 1)

            def hidden_hi(ph, j):
                act.wait_ge(htmp_ready[ph], j + 1)
                copy(hh, tmp(ph, 3 * P)).then_inc(hT_ready[ph], 1)

            def shared_silu(ph, j):
                if j > 0:
                    act.wait_ge(hT_ps[ph], j)
                silu(ph, j)
                if j > 0:
                    hidden_hi(ph, j - 1)

            def block_T(b):
                act.wait_ge(xbT_ps, b + 1)
                copy(xbT[:], ps[:, 7, :].rearrange("p (k t) -> p k t", k=KC)).then_inc(xbT_ready, 1)

            shared_silu(0, 0)
            norm2_T(TT - 1)
            rows_hi(EARLY)
            shared_silu(0, 1)
            act.wait_ge(logit_done, TT)
            nc.scalar.activation(sc, ps[:, 6, 0:TT * E], ACT.Sigmoid).then_inc(sig_done, 1)
            for j in range(2, J0):
                shared_silu(0, j)
            hidden_hi(0, J0 - 1)
            block_T(0)
            silu(0, J0)
            block_T(1)
            last_b = act.value_load(trip[0:1, 0:1], min_val=TMIN - 1, max_val=NB - 1)
            with act.Fori(1, last_b + 1) as b:
                hidden_T(b + (J0 - 1))
                silu(0, b + J0)
                block_T(b + 1)
            hidden_T(last_b + J0)
            shared_silu(1, 0)
            rows_hi(TT - 1)
            for j in range(1, LATE):
                shared_silu(1, j)
            act.wait_ge(hT_ps[1], LATE)
            hidden_hi(1, LATE - 1)

        @block.vector
        def _(dve):
            v = nc.vector
            steps = [0]

            def link(ins):
                steps[0] += 1
                ins.then_inc(dve_step, 1)
                dve.wait_ge(dve_step, steps[0])

            dve.wait_ge(l_x, 16)
            v.tensor_copy(pT.rearrange("p (b n) -> p b n", n=NPOS), praw.rearrange("p (n b) -> p b n", n=NPOS))\
                .then_inc(patch_ready, 1)

            def mean_var(i):
                link(v.bn_stats(stats[:, i % 2, :], hres[:, i, :]))
                v.bn_aggr(mv[:, i, :], stats[:, i % 2, :]).then_inc(stats_ready, 1)

            def embed(i):
                dve.wait_ge(tok_done, i + 1)
                if i == 0:
                    dve.wait_ge(l_tokb, 16)
                v.tensor_tensor(hres[:, i, :], ps[:, tok_bank(i), :], tokb, ALU.add).then_inc(tok_used, 1)
                dve.wait_ge(tok_used, i + 1)
                mean_var(i)

            def normed(i, nth, done):
                dve.wait_ge(rstd_ready, nth + 1)
                v.tensor_scalar(xn[:, i, :], hres[:, i, :], mv[:, i, 0:1], rstd[:, i:i + 1],
                                ALU.subtract, ALU.mult).then_inc(done, 1)

            def rotate(i):
                dve.wait_ge(qk_done, i + 1)
                if i == 0:
                    dve.wait_ge(l_rope, 16)
                if i >= 1:
                    dve.wait_ge(qkr_ready, i)
                b = proj_bank(i)
                half, n = HD // 2, QKV // 2 // HD

                def table(c, d0, d1, h):
                    return rope[:, i, c, d0:d1].unsqueeze(1).to_broadcast([P, h, d1 - d0])

                for c, h0, h1 in ((0, 0, n), (1, n, QK // HD)):
                    h = h1 - h0
                    src = ps[:, b + c, 0:h * HD].rearrange("p (h d) -> p h d", d=HD)
                    A, B = (x[:, h0 * HD:h1 * HD].rearrange("p (h d) -> p h d", d=HD) for x in (ropeA, ropeB))
                    v.tensor_tensor(A, src, table(0, 0, HD, h), ALU.mult)
                    v.tensor_tensor(B[:, :, 0:half], src[:, :, half:HD], table(1, 0, half, h), ALU.mult)
                    last = v.tensor_tensor(B[:, :, half:HD], src[:, :, 0:half], table(1, half, HD, h), ALU.mult)
                last.then_inc(rope_ready, 1)

            embed(0)
            embed(1)
            normed(0, 0, xn_ready)
            normed(1, 1, xn_ready)
            embed(2)
            embed(3)
            normed(2, 2, xn_ready)
            embed(4)
            normed(3, 3, xn_ready)
            normed(4, 4, xn_ready)
            def split_weights(m):
                for n in range(chunks[0], chunks[0] + m):
                    c = n % len(WCH)
                    if c == 0:
                        dve.wait_ge(l_slot[n // len(WCH)], 32)
                    if n >= 2:
                        dve.wait_ge(wh_ready, n - 1)
                    w, lo = wchunk(n // len(WCH), c, f32), wchunk(lo_early[n // len(WCH)], c, parts)
                    t = wtmp[n % 2][0:w.shape[0], 0:w.shape[1]]
                    v.tensor_scalar(t.bitcast(I32), w.bitcast(I32), HI_BITS, None, ALU.bitwise_and)\
                        .then_inc(wtmp_ready, 1)
                    if n >= len(WCH):
                        dve.wait_ge(wtmp_ready, n + 1)
                        v.tensor_tensor(lo, w, t, ALU.subtract).then_inc(wl_ready[1], 1)
                chunks[0] += m

            def split_rows(i):
                dve.wait_ge(x2T_ready, i + 1)
                if i >= 1:
                    dve.wait_ge(xh_ready, i)
                    dve.wait_ge(xl_ready, i)
                x, t = xn2T[:, :, i * P:(i + 1) * P], tmp(i == TT - 1, D).rearrange("p (k t) -> p k t", k=KC)
                v.tensor_scalar(t.bitcast(I32), x.bitcast(I32), HI_BITS, None, ALU.bitwise_and).then_inc(xtmp_ready, 1)
                dve.wait_ge(xtmp_ready, i + 1)
                v.tensor_tensor(xl(i), x, t, ALU.subtract).then_inc(xl_ready, 1)

            chunks = [0]
            for i in range(TT - 1):
                rotate(i)
                split_weights(W_SPLITS[i])

            def spread_k(a):
                n, t = AG[a], TG * a * GQ
                dve.wait_ge(qkT_ready, tiles_of(a))
                if a >= 2:
                    dve.wait_ge(s_done, a - 1)
                src = bass.AP(KT.tensor, KT.offset + t, [list(KT.ap[0]), [GQ, n], [0, NKV], [1, GK]])
                v.tensor_tensor(KD[a % 2][:, 0:n * P].rearrange("p (j n k) -> p j n k", j=n, k=GK), src, head_mask(n),
                                ALU.mult).then_inc(kd_ready, 1)

            def head_mask(n):
                return bass.AP(headm.tensor, headm.offset, [list(headm.ap[0]), [0, n], [1, NKV], [0, GK]])

            def cols(x):
                return x.rearrange("p (c k) -> p c k", k=GK)

            def soft_a(a):
                n = AG[a] * NKV
                dve.wait_ge(s_done, a + 1)
                s = cols(ps[0:QROWS, a % 2, 0:n * GK])
                link(v.tensor_reduce(nmax[0:QROWS, a % 2, 0:n], s, AX.X, ALU.max))
                if a >= 2:
                    dve.wait_ge(pT_ps, a - 1)
                v.tensor_tensor(cols(prob[a % 2][0:QROWS, 0:n * GK]), s,
                                nmax[0:QROWS, a % 2, 0:n].unsqueeze(2).to_broadcast([QROWS, n, GK]),
                                ALU.subtract).then_inc(sub_done, 1)

            def soft_b(a):
                n = AG[a] * NKV
                dve.wait_ge(exp_done, a + 1)
                p = cols(prob[a % 2][0:QROWS, 0:n * GK])
                link(v.tensor_reduce(esum[0:QROWS, a % 2, 0:n], p, AX.X, ALU.add))
                v.reciprocal(rden[0:QROWS, a % 2, 0:n], esum[0:QROWS, a % 2, 0:n]).then_inc(rden_ready, 1)

            def residual(i):
                dve.wait_ge(wo_done, i + 1)
                v.tensor_tensor(hres[:, i, :], ps[:, 3, :], hres[:, i, :], ALU.add).then_inc(resid_done, 1)
                dve.wait_ge(resid_done, i + 1)
                mean_var(i)

            dve.wait_ge(pad_ready, 1)
            spread_k(0)
            spread_k(1)
            rotate(TT - 1)
            soft_a(0)
            spread_k(2)
            soft_a(1)
            soft_b(0)
            soft_b(1)
            for a in range(AT):
                if a + 2 < AT:
                    soft_a(a + 2)
                    if a + 3 < AT:
                        spread_k(a + 3)
                    soft_b(a + 2)
                if a >= 2:
                    residual(a - 2)
                split_weights(W_SPLITS[TT - 1 + a])
                if a >= 2:
                    normed(a - 2, TT + a - 2, xn2_ready)
                if a >= 4:
                    split_rows(a - 4)
            split_rows(AT - 4)
            split_weights(W_SPLITS[-1])
            residual(TT - 1)
            normed(TT - 1, 2 * TT - 1, xn2_ready)

            def grid(x):
                return x.rearrange("p (i e) -> p i e", e=E)

            def over_experts(x):
                return x.unsqueeze(2).to_broadcast([P, TT, E])

            def over_tiles(x):
                return x.unsqueeze(1).to_broadcast([P, TT, E])

            def hidden(ph, j):
                dve.wait_ge(u_done[ph], j + 1)
                dve.wait_ge(silu_done[ph], j + 1)
                v.tensor_tensor(hg[:, 0:H], ps[:, late_bank(ph, j) + 1, 0:H], hg[:, 0:H], ALU.mult).then_inc(h_done[ph], 1)

            def split_hidden(ph, j):
                dve.wait_ge(hT_ps[ph], j + 1)
                if j >= 1:
                    dve.wait_ge(hT_ready[ph], j)
                    dve.wait_ge(hl_ready[ph], j)
                else:
                    dve.wait_ge(xh_ready, (EARLY + 1, TT)[ph])
                    dve.wait_ge(xl_ready, (EARLY + 1, TT)[ph])
                h, t = ps[:, 4, 0:3 * P], tmp(ph, 3 * P)
                v.tensor_scalar(t.bitcast(I32), h.bitcast(I32), HI_BITS, None, ALU.bitwise_and)\
                    .then_inc(htmp_ready[ph], 1)
                dve.wait_ge(htmp_ready[ph], j + 1)
                v.tensor_tensor(hl, h, t, ALU.subtract).then_inc(hl_ready[ph], 1)

            def shared_y(ph, i):
                dve.wait_ge(y_done[ph], i + 1)
                t = i + EARLY * ph
                v.tensor_tensor(hres[:, t, :], ps[:, 5, :], hres[:, t, :], ALU.add).then_inc(y_used[ph], 1)

            def expert_y(b, stored):
                dve.wait_ge(y_done[0], b + (EARLY + 1))
                dve.wait_ge(y_stored, stored)
                v.tensor_copy(yb[:], ps[:, 5, :]).then_inc(y_used[0], 1)

            hidden(0, 0)
            split_rows(EARLY)
            split_hidden(0, 0)
            hidden(0, 1)
            dve.wait_ge(sig_done, 1)
            link(v.tensor_tensor(grid(sbias), grid(sc), over_tiles(gb[:]), ALU.add))
            for sel, m, r in ((sel1, m1, r1), (sel2, m2, r2)):
                link(v.tensor_reduce(m, grid(sbias), AX.X, ALU.max))
                link(v.tensor_tensor(grid(t0), grid(sbias), over_experts(m), ALU.is_equal))
                link(v.tensor_tensor(grid(t0), grid(t0), over_tiles(rev), ALU.mult))
                link(v.tensor_reduce(r, grid(t0), AX.X, ALU.max))
                link(v.tensor_tensor(grid(sel), over_tiles(rev), over_experts(r), ALU.is_equal))
                if sel is sel1:
                    link(v.scalar_tensor_tensor(out=sbias, in0=sel1, scalar=NEG, in1=sbias, op0=ALU.mult, op1=ALU.add))
            v.tensor_tensor(msel, sel1, sel2, ALU.add).then_inc(sel_ready, 1)

            split_hidden(0, 1)
            hidden(0, 2)
            dve.wait_ge(rank_done, 1)
            tot = ps[:, 7, TT * E:2 * TT * E]
            link(v.tensor_reduce(cnt, tot.rearrange("p (i e) -> p e i", e=E), AX.X, ALU.add))
            ov = over.rearrange("p (e i) -> p e i", i=TT)
            link(v.tensor_tensor(ov, cnt.unsqueeze(2).to_broadcast([P, E, TT]),
                                 thr.unsqueeze(1).to_broadcast([P, E, TT]), ALU.is_gt))
            link(v.tensor_reduce(nblk, ov, AX.X, ALU.add))
            link(v.tensor_tensor_scan(incl, cst[:, C_ONE:C_ONE + E], nblk, 0.0, ALU.mult, ALU.add))
            link(v.tensor_tensor(base0, incl, nblk, ALU.subtract))
            bt = grid(baseT)
            link(v.tensor_scalar(bt[:, 0, :], base0, float(P), None, ALU.mult))
            for i in range(1, TT):
                link(v.tensor_tensor(bt[:, i, :], bt[:, i - 1, :], grid(tot)[:, i - 1, :], ALU.add))
            link(v.tensor_tensor(pos, ps[:, 7, 0:TT * E], baseT, ALU.add))
            for t, sel, c in ((t0, sel1, 0), (t1, sel2, 1)):
                link(v.tensor_tensor(t, pos, sel, ALU.mult))
                link(v.tensor_reduce(slotf[:, c * TT:(c + 1) * TT], grid(t), AX.X, ALU.add))
            v.tensor_copy(slot_i[:].rearrange("p c i -> p (c i)"), slotf).then_inc(slot_ready, 1)
            shared_y(0, 0)
            split_hidden(0, 2)
            hidden(0, 3)
            for t, sel, c in ((t0, sel1, 0), (t1, sel2, 1)):
                link(v.tensor_tensor(t, sc, sel, ALU.mult))
                link(v.tensor_reduce(wtop[:, c, :], grid(t), AX.X, ALU.add))
            link(v.tensor_tensor(wsum, wtop[:, 0, :], wtop[:, 1, :], ALU.add))
            link(v.reciprocal(wsum, wsum))
            link(v.tensor_tensor(wtop[:], wtop[:], wsum.unsqueeze(1).to_broadcast([P, 2, TT]), ALU.mult))
            bc = blkc.rearrange("p (b e) -> p b e", e=E)[0:1]
            link(v.tensor_tensor(bc, incl[0:1].unsqueeze(1).to_broadcast([1, NB + 1, E]),
                                 blki[0:1].unsqueeze(2).to_broadcast([1, NB + 1, E]), ALU.is_le))
            link(v.tensor_reduce(blkf[0:1], bc, AX.X, ALU.add))
            link(v.tensor_scalar(blkf[0:1], blkf[0:1], float(E - 1), None, ALU.min))
            link(v.tensor_copy(blk[:], blkf[0:1]))
            link(v.tensor_scalar(blkc[0:1, 0:NB + 1], blkf[0:1], float(WRAP), float(PLACES[WRAP] - PLACES[0] - WRAP),
                                 ALU.is_ge, ALU.mult))
            link(v.scalar_tensor_tensor(out=place[:], in0=blkf[0:1], scalar=float(PLACES[0] - SH), in1=blkc[0:1, 0:NB + 1],
                                        op0=ALU.add, op1=ALU.add))
            link(v.tensor_scalar(trip[0:1, 1:2], incl[0:1, 1:2], float(EARLY), None, ALU.add))
            v.tensor_scalar(trip[0:1, 0:1], incl[0:1, E - 1:E], -1.0, None, ALU.add).then_inc(blk_ready, 1)

            split_hidden(0, 3)
            for j in range(4, J0):
                hidden(0, j)
                if j % SH == 0:
                    shared_y(0, j // SH - 1)
                split_hidden(0, j)
            hidden(0, J0)
            shared_y(0, EARLY - 1)
            dve.wait_ge(blk_ready, 1)
            last_b = dve.value_load(trip[0:1, 0:1], min_val=TMIN - 1, max_val=NB - 1)
            hidden(0, J0 + 1)
            dve.wait_ge(y_done[0], EARLY + 1)
            v.tensor_copy(yb[:], ps[:, 5, :]).then_inc(y_used[0], 1)
            with dve.Fori(2, last_b + 1) as b:
                hidden(0, b + J0)
                expert_y(b - 1, (b - 1) * 16)
            expert_y(last_b, last_b * 16)
            hidden(1, 0)

            def combine(i, choices=(0, 1)):
                if i == 0:
                    dve.wait_ge(y_used[0], EARLY)
                if i == EARLY:
                    dve.wait_ge(y_used[1], 1)
                dve.wait_ge(gathered[i], 32)
                for c in choices:
                    ins = v.scalar_tensor_tensor(out=hres[:, i, :], in0=yg[:, c, i, :], scalar=wtop[:, c, i:i + 1],
                                                 in1=hres[:, i, :], op0=ALU.mult, op1=ALU.add)
                    if c == 0 or i == TT - 1:
                        link(ins)
                    else:
                        ins.then_inc(out_ready, 1)

            dve.wait_ge(xbT_ps, last_b + 2)
            split_rows(TT - 1)
            split_hidden(1, 0)
            hidden(1, 1)
            split_hidden(1, 1)
            combine(0)
            hidden(1, 2)
            shared_y(1, 0)
            combine(1)
            split_hidden(1, 2)
            combine(2)
            hidden(1, 3)
            combine(3, (0,))
            split_hidden(1, 3)
            combine(3, (1,))
            combine(4)
            dve.wait_ge(y_done[1], 2)
            v.tensor_tensor(hres[:, TT - 1, :], ps[:, 5, :], hres[:, TT - 1, :], ALU.add).then_inc(out_ready, 1)

        @block.gpsimd
        def _(pool):
            g = nc.gpsimd
            steps = [0]
            g.memset(halfneg[:], -0.5).then_inc(const_ready, 1)
            g.memset(xb[:], 0.0).then_inc(zero_ready, 1)
            g.memset(hg[:, H:3 * P], 0.0)
            g.memset(QT[:, NGRP * TOK:NGRP * TOKP], 0.0)
            g.memset(KT[:, TOK:TOKP], 0.0)
            g.memset(VT[:, TOK:TOKP], 0.0).then_inc(pad_ready, 1)
            pool.wait_ge(const_ready, 1)

            def inv_std(i, nth):
                pool.wait_ge(stats_ready, nth + 1)
                g.tensor_scalar(rstd[:, i:i + 1], mv[:, i, 1:2], EPS, None, ALU.add).then_inc(pool_step, 1)
                steps[0] += 1
                pool.wait_ge(pool_step, steps[0])
                g.tensor_tensor(rstd[:, i:i + 1], rstd[:, i:i + 1], halfneg[:], ALU.pow).then_inc(rstd_ready, 1)

            def rotate(i):
                pool.wait_ge(rope_ready, i + 1)
                if i >= 2:
                    pool.wait_ge(ropeT_ps, i - 1)
                g.tensor_tensor(qkv[i % 2][:, 0:QK], ropeA, ropeB, ALU.add).then_inc(qkr_ready, 1)

            for i in range(TT):
                inv_std(i, i)
            def split_weights(m):
                for n in range(chunks[0], min(chunks[0] + m, len(WCH))):
                    pool.wait_ge(wtmp_ready, n + 1)
                    w = wchunk(0, n, f32)
                    g.tensor_tensor(wchunk(lo_early[0], n, parts), w, wtmp[n % 2][0:w.shape[0], 0:w.shape[1]],
                                    ALU.subtract).then_inc(wl_ready[0], 1)
                chunks[0] += m

            chunks = [0]
            for i in range(TT - 1):
                rotate(i)
                split_weights(W_SPLITS[i])

            def spread_v(a):
                n, t = AG[a], TG * a * GQ
                pool.wait_ge(qkT_ready, tiles_of(a))
                if a >= 2:
                    pool.wait_ge(vB_ps, a - 1)
                src = bass.AP(VT.tensor, VT.offset + t, [list(VT.ap[0]), [GQ, n], [0, NKV], [1, GK]])
                own = bass.AP(headm.tensor, headm.offset, [list(headm.ap[0]), [0, n], [1, NKV], [0, GK]])
                g.tensor_tensor(VD[a % 2][:, 0:n * P].rearrange("p (j n k) -> p j n k", j=n, k=GK), src, own,
                                ALU.mult).then_inc(vd_ready, 1)

            def normalise(a):
                n = AG[a] * NKV
                pool.wait_ge(rden_ready, a + 1)
                p = prob[a % 2][0:QROWS, 0:n * GK].rearrange("p (c k) -> p c k", k=GK)
                g.tensor_tensor(p, p, rden[0:QROWS, a % 2, 0:n].unsqueeze(2).to_broadcast([QROWS, n, GK]), ALU.mult)\
                    .then_inc(prob_ready, 1)

            pool.wait_ge(pad_ready, 1)
            pool.wait_ge(l_cst, 16)
            spread_v(0)
            spread_v(1)
            rotate(TT - 1)
            normalise(0)
            normalise(1)
            for a in range(AT):
                if a + 2 < AT:
                    spread_v(a + 2)
                    normalise(a + 2)
                if a >= 2:
                    inv_std(a - 2, TT + a - 2)
            inv_std(TT - 1, 2 * TT - 1)

            pool.wait_ge(zeroed, 32)
            pool.wait_ge(slot_ready, 1)
            for c in range(2):
                for i in range(TT):
                    g.indirect_dma_start(out=x_disp, out_offset=bass.IndirectOffsetOnAxis(
                        ap=slot_i[:, c, i:i + 1].bitcast(U32), axis=0), in_=xn[:, i, :], in_offset=None)\
                        .then_inc(scattered, 16)
            def load_chunk(s, w, n, done):
                src, c0 = (wb[w] if n == len(WCH) - 1 else wa[w]), sum(WCH[:n])
                pool.dma_start(wchunk(s, n, f32), src if n == len(WCH) - 1 else src[:, c0:c0 + WCH[n]]).then_inc(done, 16)

            for e, s in enumerate(PLACES):
                if s == EARLY_SLOT or e >= WRAP:
                    pool.wait_ge(u_done[0], J0) if s == EARLY_SLOT else pool.wait_ge(y_done[0], EARLY)
                    for n in range(len(WCH)):
                        if n >= 2:
                            pool.wait_ge(l_last[e][n % 2], n // 2 * 16)
                        load_chunk(s, SH + e, n, l_last[e][n % 2])
                    pool.wait_ge(l_last[e][0], (len(WCH) + 1) // 2 * 16)
                    pool.wait_ge(l_last[e][1], len(WCH) // 2 * 16)
                else:
                    pool.wait_ge(l_slot[s], 32)
                pool.sem_inc(experts_loaded, 1)
            units = pool.value_load(trip[0:1, 1:2], min_val=EARLY, max_val=EARLY + NB)
            pool.wait_ge(y_done[0], units)
            pool.sem_inc(two_through, 1)
            pool.wait_ge(two_through, 1)
            pool.wait_ge(wh_ready, SH * len(WCH))
            loads = [(s, n) for s in range(SH) for n in range(len(WCH))]

            def load_again(i):
                s, n = loads[i]
                load_chunk(lo_late[s], s, n, l_again[i % 2])

            load_again(0)
            for i, (s, n) in enumerate(loads):
                if i + 1 < len(loads):
                    load_again(i + 1)
                pool.wait_ge(l_again[i % 2], (i // 2 + 1) * 16)
                g.tensor_tensor(wchunk(lo_late[s], n, parts), wchunk(lo_late[s], n, f32),
                                wchunk(s, n, parts).bitcast(F32), ALU.subtract).then_inc(late_wl_ready, 1)
            pool.wait_ge(all_stored, 1)
            for i in range(TT):
                for c in range(2):
                    g.indirect_dma_start(out=yg[:, c, i, :], out_offset=None, in_=y_disp,
                                         in_offset=bass.IndirectOffsetOnAxis(
                                             ap=slot_i[:, c, i:i + 1].bitcast(U32), axis=0)).then_inc(gathered[i], 16)


def constants():
    c = np.zeros((P, C_END), np.float32)
    i = np.arange(P)
    c[:, C_ID:C_ID + P] = i[:, None] == i[None, :]
    c[:, C_TRI:C_TRI + P] = i[:, None] < i[None, :]
    c[:, C_ONE:C_ONE + P] = 1.0
    q, k = np.arange(QROWS) // NGRP, np.arange(GK)
    c[:QROWS, C_MASK:C_MASK + GK] = np.where(q[:, None] // NPOS == k[None, :] // NPOS, 0.0, NEG)
    c[:, C_HEAD:C_HEAD + NKV] = i[:, None] // HD == np.arange(NKV)[None, :]
    c[:, C_REV:C_REV + E] = E - np.arange(E)
    c[:, C_THR:C_THR + TT] = P * np.arange(TT)
    c[:, C_BLK:C_BLK + NB + 1] = np.arange(NB + 1)
    freqs = (1.0 / THETA ** (np.arange(0, HD, 2, dtype=np.float32) / HD)).astype(np.float32)
    emb = np.outer(np.arange(NPOS, dtype=np.float32), freqs).astype(np.float32)
    cos, sin = np.cos(emb), np.sin(emb)
    root = float(HD) ** -0.25
    table = np.stack([np.concatenate([cos, cos], 1), np.concatenate([-sin, sin], 1)], 1) * root
    rows = table[np.arange(TOK) % NPOS].reshape(TT, P, 2 * HD)
    c[:, C_ROPE:C_END] = rows.transpose(1, 0, 2).reshape(P, TT * 2 * HD)
    return c


def kernel(x, L0_tok_W, L0_tok_b, L0_attn_Wq, L0_attn_Wk, L0_attn_Wv, L0_attn_Wo, L0_ffn_gate_w,
           L0_ffn_gate_bias, L0_ffn_shared_gw, L0_ffn_shared_dw, L0_ffn_up_w, L0_ffn_down_w):
    import concourse.bacc as bacc
    from concourse.bass_utils import run_bass_kernel_spmd

    a = {n: np.asarray(v) for n, v in dict(
        x=x, tw=L0_tok_W, tb=L0_tok_b, wq=L0_attn_Wq, wk=L0_attn_Wk, wv=L0_attn_Wv, wo=L0_attn_Wo,
        gw=L0_ffn_gate_w, gb=L0_ffn_gate_bias, sg=L0_ffn_shared_gw, sd=L0_ffn_shared_dw, up=L0_ffn_up_w,
        dn=L0_ffn_down_w).items()}

    def chunks(m):
        return m.reshape(-1, P, m.shape[1]).transpose(1, 0, 2)

    wq = a["wq"].reshape(D, NKV, NGRP, HD).transpose(0, 2, 1, 3).reshape(D, D)
    wqkv = chunks(np.concatenate([wq, a["wk"], a["wv"]], 1))
    wo = a["wo"].reshape(NKV, NGRP, HD, D).transpose(0, 2, 1, 3).reshape(P, NGRP, D)
    ups = [np.concatenate([a["sg"][(SH + s) * H:(SH + s + 1) * H], a["sg"][s * H:(s + 1) * H]]) for s in range(SH)]
    dns = [a["sd"][:, s * H:(s + 1) * H] for s in range(SH)]
    ups += [a["up"][e] for e in range(E)]
    dns += [a["dn"][e] for e in range(E)]
    wa = np.stack([np.concatenate([chunks(u.T).reshape(P, UPW), chunks(d.T[:2 * P]).reshape(P, 2 * D)], 1)
                   for u, d in zip(ups, dns)])
    wb = np.stack([d.T[2 * P:] for d in dns])
    ins = [("xT", a["x"][:, :, 0].T), ("tok_w", a["tw"].T), ("tok_b", a["tb"]), ("consts", constants()),
           ("wqkv", wqkv), ("wo", wo), ("gate_w", chunks(a["gw"].T)), ("gate_b", a["gb"]), ("wa", wa), ("wb", wb)]

    nc = bacc.Bacc("TRN2", target_bir_lowering=False, num_devices=1)
    arrays, args = {}, []
    for name, v in ins:
        v = np.ascontiguousarray(v)
        arrays[name + "_in"] = v
        args.append(nc.dram_tensor(name + "_in", v.shape, mybir.dt.from_np(v.dtype), kind="ExternalInput").ap())
    out = nc.dram_tensor("out_0", (BATCH, NPOS, D), F32, kind="ExternalOutput").ap()
    build(nc, *args, out)
    r = run_bass_kernel_spmd(nc, [arrays], core_ids=[0])
    return r.results[0]["out_0"]
```
